# Optimizing a Trainium2 kernel written in Bass

```python
import numpy as np
import jax
import jax.numpy as jnp

def _softmax(x, axis=-1):
    return jax.nn.softmax(x, axis=axis)

def _gelu(x):
    return jax.nn.gelu(x, approximate=True)

def _silu(x):
    return jax.nn.silu(x)

def _sigmoid(x):
    return jax.nn.sigmoid(x)

def _layernorm(x, axis=-1, eps=1e-05):
    m = jnp.mean(x, axis=axis, keepdims=True)
    v = jnp.var(x, axis=axis, keepdims=True)
    return (x - m) / jnp.sqrt(v + eps)

def _scatter_add(tgt, idx, src, axis=0):
    return tgt.at[idx].add(src)

def _segment_sum(src, seg, n):
    return jax.ops.segment_sum(src, seg, n)
kernel_name = 'mk_decoder_postln_d2_seqx_r4_3867a3'

def setup_inputs(seed: int=0):
    np.random.seed(seed)
    _w = jnp.asarray

    def _rec_inputs():
        import jax
        import jax.numpy as jnp
        _rk = jax.random.key(seed)
        x = 7.22e-05 + 1 * jax.random.normal(jax.random.fold_in(_rk, 1), (4, 512, 512), jnp.float32)
        _lenS = 512 - jax.random.randint(jax.random.fold_in(_rk, 7), (4,), 0, max(1, 512 // 4) + 1, jnp.int32)
        _lenS2 = 512 - jax.random.randint(jax.random.fold_in(_rk, 8), (4,), 0, max(1, 512 // 4) + 1, jnp.int32)
        _ctx_512P = jax.random.normal(jax.random.fold_in(_rk, 11), (4, 16, 128), jnp.float32)
        _ctx_512c = jax.random.dirichlet(jax.random.fold_in(_rk, 511), 0.3 * jnp.ones((16,), jnp.float32), (4, 512))
        _ctx_512t = jnp.einsum('bsk,bkd->bsd', _ctx_512c, _ctx_512P)
        _ctx_512t = _ctx_512t * jax.lax.rsqrt(jnp.mean(jnp.square(_ctx_512t)) + 1e-12) * 0.953939
        ctx_512 = -0.000514642 + 1.00011 * (_ctx_512t + 0.3 * jax.random.normal(jax.random.fold_in(_rk, 611), (4, 512, 128), jnp.float32))
        return (x, ctx_512)
    x, ctx_512 = _rec_inputs()

    def _L0_attn_setup():
        import jax, jax.numpy as jnp
        import numpy as np
        HIDDEN = 512
        NUM_HEADS = 16
        HEAD_DIM = HIDDEN // NUM_HEADS
        key = jax.random.key(seed)
        ks = jax.random.split(key, 9)
        B, S = (2, 512)
        std = HIDDEN ** (-0.5)
        return {'hidden_states': jax.random.normal(ks[0], (B, S, HIDDEN), dtype=jnp.float32), 'Wq': jax.random.normal(ks[1], (HIDDEN, HIDDEN), dtype=jnp.float32) * std, 'bq': jnp.zeros((HIDDEN,), dtype=jnp.float32), 'Wk': jax.random.normal(ks[2], (HIDDEN, HIDDEN), dtype=jnp.float32) * std, 'bk': jnp.zeros((HIDDEN,), dtype=jnp.float32), 'Wv': jax.random.normal(ks[3], (HIDDEN, HIDDEN), dtype=jnp.float32) * std, 'bv': jnp.zeros((HIDDEN,), dtype=jnp.float32), 'Wo': jax.random.normal(ks[4], (HIDDEN, HIDDEN), dtype=jnp.float32) * std, 'bo': jnp.zeros((HIDDEN,), dtype=jnp.float32)}
    _L0_attn_all = _L0_attn_setup()
    _L0_attn_in = {k: v for k, v in _L0_attn_all.items() if k in ('Wq', 'bq', 'Wk', 'bk', 'Wv', 'bv', 'Wo', 'bo')}
    del _L0_attn_all

    def _L0_xattn_setup():
        import jax, jax.numpy as jnp
        import numpy as np
        import math
        NUM_Q_HEADS = 32
        NUM_KV_HEADS = 8
        key = jax.random.key(seed)
        k1, k2, k3 = jax.random.split(key, 3)
        B, S, E = (2, 512, 512)
        kv_E = NUM_KV_HEADS * (E // NUM_Q_HEADS)
        q = jax.random.normal(k1, (B, S, E), dtype=jnp.float32)
        k = jax.random.normal(k2, (B, S, kv_E), dtype=jnp.float32)
        v = jax.random.normal(k3, (B, S, kv_E), dtype=jnp.float32)
        return {'q': q, 'k': k, 'v': v}
    _L0_xattn_all = _L0_xattn_setup()
    _L0_xattn_in = {k: v for k, v in _L0_xattn_all.items() if k in ()}
    del _L0_xattn_all

    def _L0_ffn_setup():
        import jax, jax.numpy as jnp
        import numpy as np
        ACT_BITS = 8
        EPS = 1e-05

        def act_quant(x, bits=ACT_BITS):
            qb = float(2 ** (bits - 1))
            scale = qb / jnp.clip(jnp.max(jnp.abs(x), axis=-1, keepdims=True), EPS)
            xq = jnp.clip(jnp.round(x * scale), -qb, qb - 1) / scale
            return x + jax.lax.stop_gradient(xq - x)

        def weight_quant(w):
            scale = 1.0 / jnp.clip(jnp.mean(jnp.abs(w)), EPS)
            wq = jnp.clip(jnp.round(w * scale), -1.0, 1.0) / scale
            return w + jax.lax.stop_gradient(wq - w)

        def fwht(x):
            shape = x.shape
            n = shape[-1]
            x = x.reshape(-1, n)
            h = 1
            while h < n:
                x = x.reshape(-1, n // (2 * h), 2, h)
                a, b = (x[..., 0, :], x[..., 1, :])
                x = jnp.stack([a + b, a - b], axis=-2).reshape(-1, n)
                h *= 2
            return (x * (1.0 / np.sqrt(n)).astype(np.float32)).reshape(shape)

        def bitlinear(x, w):
            return jnp.einsum('bsh,oh->bso', act_quant(x), weight_quant(w))

        def h_bitlinear(x, w):
            return jnp.einsum('bsh,oh->bso', act_quant(fwht(x)), weight_quant(w))
        key = jax.random.key(seed)
        k1, k2, k3, k4 = jax.random.split(key, 4)
        H, I = (512, 2048)
        B, S = (4, 512)
        std_in = 1.0 / np.sqrt(H)
        std_mid = 1.0 / np.sqrt(I)
        return {'x': jax.random.normal(k1, (B, S, H), dtype=jnp.float32), 'w_gate': jax.random.normal(k2, (I, H), dtype=jnp.float32) * std_in, 'w_up': jax.random.normal(k3, (I, H), dtype=jnp.float32) * std_in, 'w_down': jax.random.normal(k4, (H, I), dtype=jnp.float32) * std_mid}
    _L0_ffn_all = _L0_ffn_setup()
    _L0_ffn_in = {k: v for k, v in _L0_ffn_all.items() if k in ('w_gate', 'w_up', 'w_down')}
    del _L0_ffn_all

    def _L1_attn_setup():
        import jax, jax.numpy as jnp
        import numpy as np
        B, T, D = (4, 512, 512)
        H = 16
        HD = D // H
        key = jax.random.key(seed)
        ks = jax.random.split(key, 10)
        s = 0.02
        return {'x': jax.random.normal(ks[0], (B, T, D), dtype=jnp.float32), 'Wq': jax.random.normal(ks[1], (D, D), dtype=jnp.float32) * s, 'bq': jnp.zeros((D,), dtype=jnp.float32), 'Wk': jax.random.normal(ks[2], (D, D), dtype=jnp.float32) * s, 'bk': jnp.zeros((D,), dtype=jnp.float32), 'Wv': jax.random.normal(ks[3], (D, D), dtype=jnp.float32) * s, 'bv': jnp.zeros((D,), dtype=jnp.float32), 'Wo': jax.random.normal(ks[4], (D, D), dtype=jnp.float32) * s, 'bo': jnp.zeros((D,), dtype=jnp.float32)}
    _L1_attn_all = _L1_attn_setup()
    _L1_attn_in = {k: v for k, v in _L1_attn_all.items() if k in ('Wq', 'bq', 'Wk', 'bk', 'Wv', 'bv', 'Wo', 'bo')}
    del _L1_attn_all

    def _L1_xattn_setup():
        import jax, jax.numpy as jnp
        import numpy as np
        B, N, D = (16, 512, 128)
        H = 4
        TOP_K_RATIO = 0.3
        key = jax.random.key(seed)
        k1, k2, k3, k4 = jax.random.split(key, 4)
        h = jax.random.normal(k1, (B, N, D), dtype=jnp.float32)
        adj_raw = jax.random.uniform(k2, (B, N, N), dtype=jnp.float32)
        lim = 1.0 / np.sqrt(D)
        Wq = jax.random.uniform(k3, (D, D), minval=-lim, maxval=lim, dtype=jnp.float32)
        Wk = jax.random.uniform(k4, (D, D), minval=-lim, maxval=lim, dtype=jnp.float32)
        gamma_raw = jnp.float32(-0.85)
        return {'h': h, 'adj_raw': adj_raw, 'Wq': Wq, 'Wk': Wk, 'gamma_raw': gamma_raw}
    _L1_xattn_all = _L1_xattn_setup()
    _L1_xattn_in = {k: v for k, v in _L1_xattn_all.items() if k in ('Wq', 'Wk', 'gamma_raw')}
    del _L1_xattn_all

    def _L1_ffn_setup():
        import jax, jax.numpy as jnp
        import numpy as np
        DIM = 512
        EXPERT_DIM = 256
        N_EXPERTS = 16
        TOPK = 2
        N_SHARED = 1
        B, T = (4, 512)
        key = jax.random.key(seed)
        ks = jax.random.split(key, 9)
        s = 0.02
        return {'x': jax.random.normal(ks[0], (B, T, DIM), jnp.float32), 'router_w': jax.random.normal(ks[1], (N_EXPERTS, DIM), jnp.float32) * s, 'router_bias': jnp.zeros((N_EXPERTS,), jnp.float32), 'Wu': jax.random.normal(ks[2], (N_EXPERTS, DIM, EXPERT_DIM), jnp.float32) * s, 'Wg': jax.random.normal(ks[3], (N_EXPERTS, DIM, EXPERT_DIM), jnp.float32) * s, 'Wd': jax.random.normal(ks[4], (N_EXPERTS, EXPERT_DIM, DIM), jnp.float32) * s, 'Su': jax.random.normal(ks[5], (N_SHARED, DIM, EXPERT_DIM * TOPK), jnp.float32) * s, 'Sg': jax.random.normal(ks[6], (N_SHARED, DIM, EXPERT_DIM * TOPK), jnp.float32) * s, 'Sd': jax.random.normal(ks[7], (N_SHARED, EXPERT_DIM * TOPK, DIM), jnp.float32) * s}
    _L1_ffn_all = _L1_ffn_setup()
    _L1_ffn_in = {k: v for k, v in _L1_ffn_all.items() if k in ('router_w', 'router_bias', 'Wu', 'Wg', 'Wd', 'Su', 'Sg', 'Sd')}
    del _L1_ffn_all
    return {'x': x, 'ctx_512': ctx_512, 'L0_attn_Wq': _L0_attn_in['Wq'], 'L0_attn_bq': _L0_attn_in['bq'], 'L0_attn_Wk': _L0_attn_in['Wk'], 'L0_attn_bk': _L0_attn_in['bk'], 'L0_attn_Wv': _L0_attn_in['Wv'], 'L0_attn_bv': _L0_attn_in['bv'], 'L0_attn_Wo': _L0_attn_in['Wo'], 'L0_attn_bo': _L0_attn_in['bo'], 'L0_ffn_w_gate': _L0_ffn_in['w_gate'], 'L0_ffn_w_up': _L0_ffn_in['w_up'], 'L0_ffn_w_down': _L0_ffn_in['w_down'], 'L1_attn_Wq': _L1_attn_in['Wq'], 'L1_attn_bq': _L1_attn_in['bq'], 'L1_attn_Wk': _L1_attn_in['Wk'], 'L1_attn_bk': _L1_attn_in['bk'], 'L1_attn_Wv': _L1_attn_in['Wv'], 'L1_attn_bv': _L1_attn_in['bv'], 'L1_attn_Wo': _L1_attn_in['Wo'], 'L1_attn_bo': _L1_attn_in['bo'], 'L1_xattn_Wq': _L1_xattn_in['Wq'], 'L1_xattn_Wk': _L1_xattn_in['Wk'], 'L1_xattn_gamma_raw': _L1_xattn_in['gamma_raw'], 'L1_ffn_router_w': _L1_ffn_in['router_w'], 'L1_ffn_router_bias': _L1_ffn_in['router_bias'], 'L1_ffn_Wu': _L1_ffn_in['Wu'], 'L1_ffn_Wg': _L1_ffn_in['Wg'], 'L1_ffn_Wd': _L1_ffn_in['Wd'], 'L1_ffn_Su': _L1_ffn_in['Su'], 'L1_ffn_Sg': _L1_ffn_in['Sg'], 'L1_ffn_Sd': _L1_ffn_in['Sd']}

def reference(x, ctx_512, L0_attn_Wq, L0_attn_bq, L0_attn_Wk, L0_attn_bk, L0_attn_Wv, L0_attn_bv, L0_attn_Wo, L0_attn_bo, L0_ffn_w_gate, L0_ffn_w_up, L0_ffn_w_down, L1_attn_Wq, L1_attn_bq, L1_attn_Wk, L1_attn_bk, L1_attn_Wv, L1_attn_bv, L1_attn_Wo, L1_attn_bo, L1_xattn_Wq, L1_xattn_Wk, L1_xattn_gamma_raw, L1_ffn_router_w, L1_ffn_router_bias, L1_ffn_Wu, L1_ffn_Wg, L1_ffn_Wd, L1_ffn_Su, L1_ffn_Sg, L1_ffn_Sd):
    import jax
    import jax.numpy as jnp

    def _L0_attn_ref(hidden_states, Wq, bq, Wk, bk, Wv, bv, Wo, bo):
        import jax, jax.numpy as jnp
        import numpy as np
        HIDDEN = 512
        NUM_HEADS = 16
        HEAD_DIM = HIDDEN // NUM_HEADS
        B, S, _ = hidden_states.shape
        scale = HEAD_DIM ** (-0.5)

        def split_heads(x):
            return x.reshape(B, S, NUM_HEADS, HEAD_DIM).transpose(0, 2, 1, 3)
        q = split_heads(hidden_states @ Wq.T + bq)
        k = split_heads(hidden_states @ Wk.T + bk)
        v = split_heads(hidden_states @ Wv.T + bv)
        scores = jnp.einsum('bhqd,bhkd->bhqk', q, k) * scale
        causal = jnp.tril(jnp.ones((S, S), dtype=bool))
        scores = jnp.where(causal, scores, jnp.float32(-jnp.inf))
        attn = jax.nn.softmax(scores, axis=-1)
        out = jnp.einsum('bhqk,bhkd->bhqd', attn, v)
        out = out.transpose(0, 2, 1, 3).reshape(B, S, HIDDEN)
        return out @ Wo.T + bo

    def _L0_xattn_ref(q, k, v):
        import jax, jax.numpy as jnp
        import numpy as np
        import math
        NUM_Q_HEADS = 32
        NUM_KV_HEADS = 8
        B, S, E = q.shape
        H, KV = (NUM_Q_HEADS, NUM_KV_HEADS)
        D = E // H
        G = H // KV
        scale = math.sqrt(D)
        qh = q.reshape(B, S, KV, G, D).transpose(0, 2, 3, 1, 4)
        kh = k.reshape(B, S, KV, D).transpose(0, 2, 1, 3)
        vh = v.reshape(B, S, KV, D).transpose(0, 2, 1, 3)
        scores = jnp.einsum('bkgsd,bktd->bkgst', qh, kh) / scale
        weights = jax.nn.softmax(scores, axis=-1)
        out = jnp.einsum('bkgst,bktd->bkgsd', weights, vh)
        return out.transpose(0, 3, 1, 2, 4).reshape(B, S, E)

    def _L0_ffn_ref(x, w_gate, w_up, w_down):
        import jax, jax.numpy as jnp
        import numpy as np
        ACT_BITS = 8
        EPS = 1e-05

        def act_quant(x, bits=ACT_BITS):
            qb = float(2 ** (bits - 1))
            scale = qb / jnp.clip(jnp.max(jnp.abs(x), axis=-1, keepdims=True), EPS)
            xq = jnp.clip(jnp.round(x * scale), -qb, qb - 1) / scale
            return x + jax.lax.stop_gradient(xq - x)

        def weight_quant(w):
            scale = 1.0 / jnp.clip(jnp.mean(jnp.abs(w)), EPS)
            wq = jnp.clip(jnp.round(w * scale), -1.0, 1.0) / scale
            return w + jax.lax.stop_gradient(wq - w)

        def fwht(x):
            shape = x.shape
            n = shape[-1]
            x = x.reshape(-1, n)
            h = 1
            while h < n:
                x = x.reshape(-1, n // (2 * h), 2, h)
                a, b = (x[..., 0, :], x[..., 1, :])
                x = jnp.stack([a + b, a - b], axis=-2).reshape(-1, n)
                h *= 2
            return (x * (1.0 / np.sqrt(n)).astype(np.float32)).reshape(shape)

        def bitlinear(x, w):
            return jnp.einsum('bsh,oh->bso', act_quant(x), weight_quant(w))

        def h_bitlinear(x, w):
            return jnp.einsum('bsh,oh->bso', act_quant(fwht(x)), weight_quant(w))
        gate = bitlinear(x, w_gate)
        up = bitlinear(x, w_up)
        intermediate = jax.nn.silu(gate) * up
        return h_bitlinear(intermediate, w_down)

    def _L1_attn_ref(x, Wq, bq, Wk, bk, Wv, bv, Wo, bo):
        import jax, jax.numpy as jnp
        import numpy as np
        B, T, D = (4, 512, 512)
        H = 16
        HD = D // H
        b, t, _ = x.shape

        def split_heads(y):
            return y.reshape(b, t, H, HD).transpose(0, 2, 1, 3)
        q = split_heads(x @ Wq.T + bq)
        k = split_heads(x @ Wk.T + bk)
        v = split_heads(x @ Wv.T + bv)
        scale = 1.0 / jnp.sqrt(jnp.float32(HD))
        scores = jnp.einsum('bhqd,bhkd->bhqk', q, k) * scale
        causal = jnp.triu(jnp.ones((t, t), dtype=bool), k=1)
        scores = jnp.where(causal, -jnp.inf, scores)
        attn = jax.nn.softmax(scores, axis=-1)
        ctx = jnp.einsum('bhqk,bhkd->bhqd', attn, v)
        ctx = ctx.transpose(0, 2, 1, 3).reshape(b, t, D)
        return ctx @ Wo.T + bo

    def _L1_xattn_ref(h, adj_raw, Wq, Wk, gamma_raw):
        import jax, jax.numpy as jnp
        import numpy as np
        B, N, D = (16, 512, 128)
        H = 4
        TOP_K_RATIO = 0.3
        b, n, dm = h.shape
        d = dm // H
        Q = (h @ Wq.T).reshape(b, n, H, d).transpose(0, 2, 1, 3)
        K = (h @ Wk.T).reshape(b, n, H, d).transpose(0, 2, 1, 3)
        sim = jnp.einsum('bhnd,bhmd->bnm', Q, K) / (jnp.sqrt(jnp.float32(d)) * H)
        k = max(1, int(n * TOP_K_RATIO))
        topk_vals = jax.lax.top_k(sim, k)[0]
        threshold = topk_vals[:, :, -1:]
        sparse_mask = (sim >= threshold).astype(sim.dtype)
        A_learned = jax.nn.sigmoid(sim) * sparse_mask
        A_learned = (A_learned + jnp.swapaxes(A_learned, -1, -2)) * 0.5
        gamma = jax.nn.sigmoid(gamma_raw)
        return (1.0 - gamma) * adj_raw + gamma * A_learned

    def _L1_ffn_ref(x, router_w, router_bias, Wu, Wg, Wd, Su, Sg, Sd):
        import jax, jax.numpy as jnp
        import numpy as np
        DIM = 512
        EXPERT_DIM = 256
        N_EXPERTS = 16
        TOPK = 2
        N_SHARED = 1
        B, T = (4, 512)
        Bx, Tx, D = x.shape
        flat = x.reshape(Bx * Tx, D)
        logits = flat @ router_w.T
        scores = jax.nn.softmax(logits, axis=-1)
        _, topk_idx = jax.lax.top_k(logits + router_bias, TOPK)
        topk_scores = jnp.take_along_axis(scores, topk_idx, axis=-1)
        topk_scores = topk_scores / topk_scores.sum(-1, keepdims=True)
        combine = jnp.einsum('nk,nke->ne', topk_scores, jax.nn.one_hot(topk_idx, N_EXPERTS, dtype=scores.dtype))
        out = jnp.zeros_like(flat)
        for e in range(N_EXPERTS):
            h = jax.nn.silu(flat @ Wu[e]) * (flat @ Wg[e])
            out = out + combine[:, e:e + 1] * (h @ Wd[e])
        for s in range(N_SHARED):
            out = out + jax.nn.silu(flat @ Su[s]) * (flat @ Sg[s]) @ Sd[s]
        return out.reshape(Bx, Tx, D)
    x = _layernorm(x + _L0_attn_ref(x, L0_attn_Wq, L0_attn_bq, L0_attn_Wk, L0_attn_bk, L0_attn_Wv, L0_attn_bv, L0_attn_Wo, L0_attn_bo), axis=-1)
    x = _layernorm(x + _L0_xattn_ref(x, ctx_512, ctx_512), axis=-1)
    x = _layernorm(x + _L0_ffn_ref(x, L0_ffn_w_gate, L0_ffn_w_up, L0_ffn_w_down), axis=-1)
    x = _layernorm(x + _L1_attn_ref(x, L1_attn_Wq, L1_attn_bq, L1_attn_Wk, L1_attn_bk, L1_attn_Wv, L1_attn_bv, L1_attn_Wo, L1_attn_bo), axis=-1)
    x = _layernorm(x + _L1_xattn_ref(ctx_512, x, L1_xattn_Wq, L1_xattn_Wk, L1_xattn_gamma_raw), axis=-1)
    x = _layernorm(x + _L1_ffn_ref(x, L1_ffn_router_w, L1_ffn_router_bias, L1_ffn_Wu, L1_ffn_Wg, L1_ffn_Wd, L1_ffn_Su, L1_ffn_Sg, L1_ffn_Sd), axis=-1)
    return x

_drawn_inputs = setup_inputs


def setup_inputs(seed=0):
    import zlib

    import numpy as np

    out = dict(_drawn_inputs(seed))
    spreads = {'L0_attn_bq': (0.0, 0.587),
     'L0_attn_bk': (0.0, 2.0),
     'L0_attn_bv': (0.0, 0.1),
     'L0_attn_bo': (0.0, 0.1),
     'L1_attn_bq': (0.0, 0.8),
     'L1_attn_bk': (0.0, 2.0),
     'L1_attn_bv': (0.0, 0.1),
     'L1_attn_bo': (0.0, 0.1),
     'L1_ffn_router_bias': (0.0, 1.997)}
    factors = {'L1_attn_Wq': 8.0, 'L1_attn_Wk': 8.0, 'L1_ffn_router_w': 2.893}
    for name, (base, spread) in spreads.items():
        noise = np.random.default_rng([zlib.crc32(name.encode()), seed]).standard_normal(out[name].shape)
        drawn = base * np.exp(spread * noise) if base else spread * noise
        out[name] = jnp.asarray(drawn.astype(out[name].dtype))
    for name, factor in factors.items():
        out[name] = (out[name] * factor).astype(out[name].dtype)
    return out
```

```python
import concourse.bass as bass
from concourse import mybir
from contextlib import ExitStack

F32 = mybir.dt.float32
F32R = mybir.dt.float32r
BF16 = mybir.dt.bfloat16
U32 = mybir.dt.uint32
I32 = mybir.dt.int32
ALU = mybir.AluOpType
ACT = mybir.ActivationFunctionType
AX = mybir.AxisListType

P = 128
NB = 4
S = 512
D = 512
NT = S // P
KC = D // P
BANK = 512
NEG = -3.0e38
MAGIC = 12582912.0
LN_EPS = 1e-5


class Steps:

    def __init__(self, eng, sem, turn, per):
        self.eng, self.sem, self.turn, self.per, self.n = eng, sem, turn, per, 0

    def __call__(self, inst):
        self.n += 1
        inst.then_inc(self.sem, 1)
        self.eng.wait_ge(self.sem, self.turn * self.per + self.n)

    def done(self):
        assert self.n == self.per, (self.n, self.per)


def own_semaphores(nc, ctx, tag):
    taken = []

    @ctx.callback
    def _():
        nc.clear_and_free_semaphores(taken)
        nc.all_engine_barrier()

    def sem(name):
        taken.append(nc.alloc_semaphore(name=f"{tag}_{name}"))
        return taken[-1]
    return sem


RSTD_STEPS = 25


def emit_rstd(nc, step, stats, mean, var, y, a):
    v = nc.vector
    even, odd = stats[:, :, 0:3], stats[:, :, 3:6]
    step(v.tensor_tensor(mean, even[:, :, 1], odd[:, :, 1], ALU.add))
    step(v.tensor_tensor(a, even[:, :, 1], odd[:, :, 1], ALU.subtract))
    step(v.tensor_tensor(var, even[:, :, 2], odd[:, :, 2], ALU.add))
    step(v.tensor_scalar(mean, mean, 0.5, None, ALU.mult))
    step(v.tensor_tensor(a, a, a, ALU.mult))
    step(v.tensor_scalar(var, var, 1.0 / D, LN_EPS, ALU.mult, ALU.add))
    step(v.scalar_tensor_tensor(out=var, in0=a, scalar=0.25, in1=var, op0=ALU.mult, op1=ALU.add))
    step(v.tensor_scalar(a.bitcast(I32), var.bitcast(I32), 1, None, ALU.logical_shift_right))
    step(v.tensor_scalar(y.bitcast(I32), a.bitcast(I32), -1.0, 1597463007.0, ALU.mult, ALU.add))
    for _ in range(4):
        step(v.tensor_tensor(a, y, y, ALU.mult))
        step(v.tensor_tensor(a, a, var, ALU.mult))
        step(v.tensor_scalar(a, a, -0.5, 1.5, ALU.mult, ALU.add))
        step(v.tensor_tensor(y, y, a, ALU.mult))


def emit_layernorm(nc, step, z, out, t):
    v = nc.vector
    for i in range(NT):
        step(v.bn_stats(t["stats"][:, i, :], z[:, i, :]))
    emit_rstd(nc, step, t["stats"][:], t["mean"][:], t["var"][:], t["rstd"][:], t["tmp"][:])
    for i in range(NT):
        step(v.tensor_scalar(out[:, i, :], z[:, i, :], t["mean"][:, i:i + 1], t["rstd"][:, i:i + 1],
                             ALU.subtract, ALU.mult))


LN_STEPS = RSTD_STEPS + 2 * NT


def ln_scratch(sb, tag):
    return dict(stats=sb(f"{tag}_stats", [P, NT, 6], F32), mean=sb(f"{tag}_mean", [P, NT], F32),
                var=sb(f"{tag}_var", [P, NT], F32), rstd=sb(f"{tag}_rstd", [P, NT], F32),
                tmp=sb(f"{tag}_tmp", [P, NT], F32))


def stage_self_attention(nc, tag, X, C, wts, bias_qk, bias_rows):
    H, HD = 16, 32
    VW = 64
    VP = H * (HD + 1) + VW - HD - 1
    R = 3 * HD
    G = H // 4
    SCALE = HD ** -0.5
    pe, ve, ac, gp, sy = nc.tensor, nc.vector, nc.scalar, nc.gpsimd, nc.sync
    ctx = ExitStack()
    with ctx:
        sb = lambda n, s, d: ctx.enter_context(nc.sbuf_tensor(f"{tag}_{n}", s, d))
        ps = lambda n, s: ctx.enter_context(nc.psum_tensor(f"{tag}_{n}", s, F32))
        sem = own_semaphores(nc, ctx, f"{tag}")

        WH = sb("WH", [P, 4, KC, D], F32R)
        WL = sb("WL", [P, 4, KC, D], F32R)
        XB = sb("XB", [P, NT, D], F32)
        XTH = sb("XTH", [P, KC, S], F32R)
        XTL = sb("XTL", [P, KC, S], F32R)
        HL = sb("HL", [P, 4, S], F32R)
        QKS = sb("QKS", [R + 1, 2, 2, 4, S], F32R)
        PT = sb("PT", [P, 2, 2560], F32)
        V = sb("V", [P, NT, VP], F32)
        Z = sb("Z", [P, NT, D], F32)
        BQK = sb("BQK", [P, 2, KC], F32)
        BR = sb("BR", [P, 2, D], F32)
        negm = sb("negm", [P, 4, NT], F32)
        mT = sb("mT", [4 * NT, P], F32R)
        OS = sb("OS", [P, S], F32)
        rden = sb("rden", [P, NT, 2, 1], F32)
        ln = ln_scratch(sb, "ln")
        WS = [PT[:, r, 0:KC * D].rearrange("p (k n) -> p k n", k=KC) for r in range(2)]
        M = [ps(f"M{i}", [P, 2 * BANK]) for i in range(2)]
        T = ps("T", [P, 2 * BANK])
        O = [ps(f"O{i}", [P, BANK]) for i in range(2)]

        w_in = [sem("w_in0"), sem("w_in1")]
        w_hi, w_lo, b_in = sem("w_hi"), sem("w_lo"), sem("b_in")
        ones_set = sem("ones_set")
        xb_in = sem("xb_in")
        m_full = sem("m_full")
        m_free = sem("m_free")
        hi_done = sem("hi_done")
        t_full = sem("t_full")
        t_free = sem("t_free")
        pv_full = sem("pv_full")
        o_free = sem("o_free")
        stacked = [sem("stacked0"), sem("stacked1")]
        shifted = [sem("shifted0"), sem("shifted1")]
        between = sem("between")
        norm = sem("norm")
        xbo = sem("xbo")

        SPREAD = [[1, 1, 1, 1, 2, 0]] + [[0, 0, 2, 2, 2, 0]] * 3
        MT_AT, QK_AT = [5, 5, 5, 5], 2
        plan = [("M", "xt", 0), ("M", "xt", 1), ("M", "qk", 0), ("M", "v", 0), ("M", "v", 1),
                ("M", "qk", 1)]
        plan += [("M", "max", (0, u)) for u in range(6)] + [("M", "mt", 0)]
        for g in range(G):
            spread, units = SPREAD[g], iter(range(6))
            for s in range(6):
                plan.append(("S", g, s))
                if g + 1 < G:
                    plan += [("M", "max", (g + 1, next(units))) for _ in range(spread[s])]
                    if s == MT_AT[g]:
                        plan.append(("M", "mt", g + 1))
                    if s == QK_AT and g + 2 < G:
                        plan.append(("M", "qk", g + 2))
                q = 2 * g + s // 3 - 1
                if q >= 1 and s % 3 == 0:
                    plan.append(("M", "turn", q - 1))
                if q >= 0:
                    plan.append(("P", q, s % 3))
        plan += [("M", "turn", 2 * G - 2)] + [("P", 2 * G - 1, c) for c in range(3)] + [("M", "turn", 2 * G - 1)]
        plan += [("M", "at", 0), ("M", "at", 1), ("M", "out", 0), ("M", "out", 1)]
        m_units = [x for x in plan if x[0] == "M"]
        MU = len(m_units)
        assert MU % 2 == 0
        HI = [x for x in m_units if x[1] in ("xt", "qk", "at")]
        SU, PU = 6 * G, 2 * G
        at = {(x[1], x[2]): n for n, x in enumerate(m_units)}
        hi_at = {(x[1], x[2]): n for n, x in enumerate(HI)}

        MAX_UNITS = [[(0, 3, 0), (1, 3, 512)], [(2, 3, 0), (3, 3, 512)],
                     [(0, 2, 0), (1, 2, 512)], [(2, 2, 0), (3, 2, 512)],
                     [(h, 1, 256 * h) for h in range(4)], [(h, 0, 128 * h) for h in range(4)]]
        EXP_UNITS = [[(0, 0, 0), (0, 1, 512), (0, 3, 896)], [(1, 0, 0), (1, 1, 512), (1, 3, 896)],
                     [(0, 2, 0), (1, 2, 256)]]
        PT_AT = {(h, j): 1024 * u + c for u, unit in enumerate(EXP_UNITS) for h, j, c in unit}

        block = ctx.enter_context(nc.Block())

        @block.sync
        def _(sp):
            def shift_row(g):
                sp.wait_ge(m_free, mt_due[g])
                sp.dma_start(QKS[R:R + 1, g % 2, 0, :, :].bitcast(F32).rearrange("p h (i q) -> p (h i) q", i=NT),
                             mT[:, :].bitcast(F32)).then_inc(shifted[g % 2], 16)

            sp.dma_start(BQK[:], bias_qk).then_inc(b_in, 16)
            sp.dma_start(BR[:], bias_rows).then_inc(b_in, 16)
            for w in range(4):
                if w >= 2:
                    sp.wait_ge(w_lo, w - 1)
                sp.dma_start(WS[w % 2], wts[w]).then_inc(w_in[w % 2], 16)
            sp.wait_ge(w_lo, 4)
            with sp.Fori(0, NB) as b:
                qk_due = [sp.snap(b * MU + 2 + at["qk", g] + 1) for g in range(G)]
                mt_due = [sp.snap(b * MU + 2 + at["mt", g] + 1) for g in range(G)]
                scores_due = [None, None] + [sp.snap(b * SU + 6 * (g - 1)) for g in range(2, G)]
                for g in range(G):
                    r = g % 2
                    if g >= 2:
                        shift_row(g - 1)
                    sp.wait_ge(m_free, qk_due[g])
                    if g >= 2:
                        sp.sem_inc(between, 1)
                        sp.wait_ge(t_full, scores_due[g])
                    for h in range(4):
                        rows = slice(HD * h, HD * h + HD)
                        sp.dma_start(QKS[0:HD, r, :, h, :].bitcast(F32), HL[rows, 1:3, :].bitcast(F32)).then_inc(stacked[r], 16)
                        sp.dma_start(QKS[HD:2 * HD, r, :, h, :].bitcast(F32), HL[rows, 1:4:2, :].bitcast(F32)).then_inc(stacked[r], 16)
                        sp.dma_start(QKS[2 * HD:3 * HD, r, :, h, :].bitcast(F32), HL[rows, 0:3:2, :].bitcast(F32)).then_inc(stacked[r], 16)
                    if g == 1:
                        shift_row(0)
                shift_row(G - 1)

        @block.gpsimd
        def _(pool):
            pool.memset(V[:, :, H * (HD + 1):], 0.0).then_inc(ones_set, 1)
            pool.wait_ge(ones_set, 1)
            pool.memset(V[:, :, 0:H * (HD + 1)].rearrange("p i (h d) -> p i h d", h=H)[:, :, :, HD], 1.0).then_inc(ones_set, 1)
            pool.wait_ge(ones_set, 2)
            pool.memset(QKS[R:R + 1, :, 1, :, :].bitcast(F32), 1.0).then_inc(ones_set, 1)
            pool.wait_ge(b_in, 32)
            with pool.Fori(0, NB) as b:
                pool.dma_start(XB[:], X[:, b, :, :]).then_inc(xb_in, 16)
                pool.wait_ge(m_free, b * MU + 2 + at["at", 1] + 1)
                for i in range(NT):
                    gp.tensor_tensor(Z[:, i, :], XB[:, i, :], BR[:, 1, :], ALU.add).then_inc(xbo, 1)
                    pool.wait_ge(xbo, b * NT + i + 1)

        @block.scalar
        def _(act):
            for w in range(4):
                act.wait_ge(w_in[w % 2], 16 * (w // 2 + 1))
                ac.activation(WH[:, w], WS[w % 2], ACT.Copy).then_inc(w_hi, 1)
            act.wait_ge(b_in, 32)
            act.sem_inc(t_free, 1)
            act.sem_inc(o_free, 2)
            with act.Fori(0, NB) as b:
                for x in plan:
                    if x[0] == "M" and x[1] in ("xt", "qk", "at"):
                        n = at[x[1], x[2]]
                        act.wait_ge(m_full, b * MU + n + 1)
                        src = M[n % 2]
                        if x[1] != "qk":
                            dst = XTH[:, 2 * x[2]:2 * x[2] + 2, :].rearrange("p k s -> p (k s)")
                            ac.activation(dst, src[:], ACT.Identity).then_inc(hi_done, 1)
                        else:
                            c = x[2]
                            if c >= 1:
                                r = (c - 1) % 2
                                act.wait_ge(stacked[r], (b * 2 + (c - 1) // 2 + 1) * 16 * 12)
                            ac.activation(HL[:, 1, :], src[:, 0:BANK], ACT.Identity, bias=BQK[:, 0, c:c + 1])
                            ac.activation(HL[:, 2, :], src[:, BANK:], ACT.Identity,
                                          bias=BQK[:, 1, c:c + 1]).then_inc(hi_done, 1)
                    elif x[0] == "S":
                        g, s = x[1:]
                        pair = 2 * g + s // 3
                        act.wait_ge(t_full, b * SU + 6 * g + s + 1)
                        if s % 3 == 0 and pair >= 2:
                            act.wait_ge(pv_full, b * PU + pair - 1)
                        w = 512 if s % 3 == 2 else 1024
                        ac.activation(PT[:, pair % 2, 1024 * (s % 3):1024 * (s % 3) + w], T[:, 0:w],
                                      ACT.Exp, scale=SCALE).then_inc(t_free, 1)
                    elif x[0] == "P" and x[2] == 2:
                        q = x[1]
                        act.wait_ge(pv_full, b * PU + q + 1)
                        if q >= 1:
                            act.wait_ge(m_full, b * MU + at["turn", q - 1] + 1)
                        ac.activation(OS[:], O[q % 2][:], ACT.Identity).then_inc(o_free, 1)

        @block.vector
        def _(dve):
            for w in range(4):
                dve.wait_ge(w_hi, w + 1)
                ve.tensor_tensor(WL[:, w].rearrange("p k n -> p (k n)"),
                                 WS[w % 2].rearrange("p k n -> p (k n)"),
                                 WH[:, w].bitcast(F32).rearrange("p k n -> p (k n)"),
                                 ALU.subtract).then_inc(w_lo, 1)
            dve.wait_ge(b_in, 32)
            dve.sem_inc(m_free, 2)
            cut = m_units.index(("M", "mt", 1)) + 1
            STEPS = PU + LN_STEPS

            def through(b, units, step=None):
                for x in units:
                    kind, arg = x[1:]
                    n = at[kind, arg]
                    m = M[n % 2]
                    dve.wait_ge(m_full, b * MU + n + 1)
                    if kind in ("xt", "qk", "at"):
                        dve.wait_ge(hi_done, b * len(HI) + hi_at[kind, arg] + 1)
                    if kind in ("xt", "at"):
                        ks = slice(2 * arg, 2 * arg + 2)
                        last = ve.tensor_tensor(XTL[:, ks, :].rearrange("p k s -> p (k s)"), m[:],
                                                XTH[:, ks, :].bitcast(F32).rearrange("p k s -> p (k s)"),
                                                ALU.subtract)
                    elif kind == "v":
                        for j in range(2):
                            i = 2 * arg + j
                            last = ve.tensor_tensor(
                                V[:, i, 0:H * (HD + 1)].rearrange("p (h d) -> p h d", h=H)[:, :, 0:HD], m[:, BANK * j:BANK * (j + 1)].rearrange("p (h d) -> p h d", h=H),
                                BR[:, 0, :].rearrange("p (h d) -> p h d", h=H), ALU.add)
                    elif kind == "qk":
                        ve.scalar_tensor_tensor(out=HL[:, 0, :], in0=m[:, 0:BANK], scalar=BQK[:, 0, arg:arg + 1],
                                                in1=HL[:, 1, :].bitcast(F32), op0=ALU.add, op1=ALU.subtract)
                        last = ve.scalar_tensor_tensor(out=HL[:, 3, :], in0=m[:, BANK:], scalar=BQK[:, 1, arg:arg + 1],
                                                       in1=HL[:, 2, :].bitcast(F32), op0=ALU.add, op1=ALU.subtract)
                    elif kind == "max":
                        g, u = arg
                        h0, i, _ = MAX_UNITS[u][0]
                        nh = len(MAX_UNITS[u])
                        w = P * (i + 1)
                        pitch = BANK if nh == 2 else w
                        src = m[:, 0:nh * pitch].rearrange("p (h k) -> p h k", h=nh)[:, :, 0:w]
                        last = ve.tensor_reduce(negm[:, h0:h0 + nh, i], src, AX.X, ALU.max, negate=True)
                    elif kind == "mt":
                        if arg >= 1:
                            r = (arg - 1) % 2
                            dve.wait_ge(shifted[r], (b * 2 + (arg - 1) // 2 + 1) * 16)
                        last = ve.tensor_copy(mT[:, :], m[0:4 * NT, 0:P])
                    elif kind == "turn":
                        o = m[:, 0:S].rearrange("p (i h d) -> p i h d", i=NT, h=2)
                        step(ve.reciprocal(rden[:], o[:, :, :, HD:HD + 1]))
                        for h in range(2):
                            c = HD * (2 * arg + h)
                            last = ve.tensor_tensor(Z[:, :, c:c + HD], o[:, :, h, 0:HD],
                                                    rden[:, :, h].to_broadcast([P, NT, HD]), ALU.mult)
                    elif kind == "out":
                        dve.wait_ge(xbo, b * NT + NT)
                        for j in range(2):
                            i = 2 * arg + j
                            last = ve.tensor_tensor(Z[:, i, :], m[:, BANK * j:BANK * (j + 1)], Z[:, i, :], ALU.add)
                    last.then_inc(m_free, 1)
                    dve.wait_ge(m_free, b * MU + n + 3)

            def normalise(step, b):
                emit_layernorm(nc, step, Z, X[:, b, :, :], ln)
                step.done()

            through(0, m_units[:cut])
            with dve.Fori(0, NB - 1) as b:
                step = Steps(dve, norm, b, STEPS)
                through(b, m_units[cut:], step)
                through(b + 1, m_units[:cut])
                normalise(step, b)
            step = Steps(dve, norm, NB - 1, STEPS)
            through(NB - 1, m_units[cut:], step)
            normalise(step, NB - 1)

        @block.tensor
        def _(t):
            t.wait_ge(w_lo, 4)
            t.wait_ge(ones_set, 3)

            def product(out, lhs, rhs, hi_lo):
                last = len(hi_lo) - 1
                for n, (a, c) in enumerate(hi_lo):
                    inst = pe.matmul(out, lhs(a, c), rhs(a, c), start=(n == 0), stop=(n == last))
                return inst

            PASSES = [(a, k) for k in range(KC) for a in range(3)]
            first = lambda hi, lo, a: lo if a == 1 else hi
            second = lambda hi, lo, a: lo if a == 2 else hi

            with t.Fori(0, NB) as b:
                for x in plan:
                    if x[0] == "M":
                        kind, arg = x[1:]
                        n = at[kind, arg]
                        m = M[n % 2]
                        t.wait_ge(m_free, b * MU + n + 1)
                        if kind == "xt":
                            if arg == 0:
                                t.wait_ge(xb_in, b * 16 + 16)
                            for k in range(2):
                                for i in range(NT):
                                    c = P * (2 * arg + k)
                                    last = pe.transpose(m[:, BANK * k + P * i:BANK * k + P * (i + 1)],
                                                        XB[:, i, c:c + P], C["ident"][:])
                        elif kind == "at":
                            if arg == 0:
                                t.wait_ge(m_free, b * MU + 2 + at["turn", 2 * G - 1] + 1)
                            for k in range(2):
                                for i in range(NT):
                                    c = P * (2 * arg + k)
                                    last = pe.transpose(m[:, BANK * k + P * i:BANK * k + P * (i + 1)],
                                                        Z[:, i, c:c + P], C["ident"][:])
                        elif kind in ("v", "out"):
                            w = 2 if kind == "v" else 3
                            if kind == "out" and arg == 0:
                                t.wait_ge(m_free, b * MU + 2 + at["at", 1] + 1)
                            for j in range(2):
                                i = 2 * arg + j
                                last = product(m[:, BANK * j:BANK * (j + 1)],
                                               lambda a, k: first(XTH, XTL, a)[:, k, P * i:P * (i + 1)],
                                               lambda a, k: second(WH, WL, a)[:, w, k, :], PASSES)
                        elif kind == "qk":
                            cols = slice(P * arg, P * (arg + 1))
                            if arg == 0:
                                t.wait_ge(m_free, b * MU + 2 + at["xt", 1] + 1)
                            for w in range(2):
                                last = product(m[:, BANK * w:BANK * (w + 1)],
                                               lambda a, k: first(WH, WL, a)[:, w, k, cols],
                                               lambda a, k: second(XTH, XTL, a)[:, k, :], PASSES)
                        elif kind == "max":
                            g, u = arg
                            r = g % 2
                            if u == 0:
                                t.wait_ge(stacked[r], (b * 2 + g // 2 + 1) * 16 * 12)
                            for h, i, c in MAX_UNITS[u]:
                                w = P * (i + 1)
                                pe.matmul(m[:, c:c + w], QKS[0:R, r, 0, h, P * i:P * (i + 1)],
                                          QKS[0:R, r, 1, h, 0:w], start=True, stop=False)
                                last = pe.matmul(m[:, c + P * i:c + w], C["identr"][:], C["mask_qk"][:],
                                                 start=False, stop=True)
                        elif kind == "mt":
                            t.wait_ge(m_free, b * MU + 2 + at["max", (arg, 5)] + 1)
                            last = pe.transpose(m[0:4 * NT, 0:P], negm[:].rearrange("p h i -> p (h i)"),
                                                C["ident"][:])
                        elif kind == "turn":
                            t.wait_ge(o_free, b * PU + arg + 3)
                            for i in range(NT):
                                last = pe.transpose(m[:, P * i:P * (i + 1)], OS[:, P * i:P * (i + 1)],
                                                    C["ident"][:])
                        last.then_inc(m_full, 1)
                    elif x[0] == "S":
                        g, s = x[1:]
                        r = g % 2
                        if s == 0:
                            t.wait_ge(shifted[r], (b * 2 + g // 2 + 1) * 16)
                        t.wait_ge(t_free, b * SU + 6 * g + s + 1)
                        for hp, j, c in EXP_UNITS[s % 3]:
                            h = 2 * (s // 3) + hp
                            w = S - P * j
                            pe.matmul(T[:, c:c + w], QKS[0:R + 1, r, 1, h, P * j:P * (j + 1)],
                                      QKS[0:R + 1, r, 0, h, P * j:S], start=True, stop=False)
                            last = pe.matmul(T[:, c:c + P], C["identr"][:], C["mask_kq"][:],
                                             start=False, stop=True)
                        last.then_inc(t_full, 1)
                    else:
                        q, part = x[1:]
                        o = O[q % 2]
                        if part == 0:
                            t.wait_ge(o_free, b * PU + q + 1)
                            t.wait_ge(t_free, b * SU + 3 * (q + 1) + 1)
                        blocks = [(h, j) for h in range(2) for j in range(NT)]
                        for h, j in blocks[[0, 3, 6][part]:[3, 6, 8][part]]:
                            w = S - P * j
                            last = pe.matmul(o[VW * h:VW * (h + 1), P * j:S], V[:, j, (HD + 1) * (2 * q + h):(HD + 1) * (2 * q + h) + VW],
                                             PT[:, q % 2, PT_AT[h, j]:PT_AT[h, j] + w],
                                             start=(j == 0), stop=(j == NT - 1))
                        if part == 2:
                            last.then_inc(pv_full, 1)


def stage_cross_attention(nc, X, C, A):
    H, KV, HD = 32, 8, 16
    VW = 32
    R = 3 * HD
    G = KV
    SCALE = 1.0 / (HD ** 0.5)
    E = KV * HD
    pe, ve, ac, gp = nc.tensor, nc.vector, nc.scalar, nc.gpsimd
    ctx = ExitStack()
    with ctx:
        sb = lambda n, s, d: ctx.enter_context(nc.sbuf_tensor(f"x0_{n}", s, d))
        ps = lambda n, s: ctx.enter_context(nc.psum_tensor(f"x0_{n}", s, F32))
        sem = own_semaphores(nc, ctx, f"x0")

        XB = sb("XB", [P, NT, D], F32)
        XTH = sb("XTH", [P, KC, S], F32R)
        XTL = sb("XTL", [P, KC, S], F32R)
        CB = sb("CB", [P, S], F32)
        CH = sb("CH", [P, S], F32R)
        CL = sb("CL", [P, S], F32R)
        CTOK = sb("CTOK", [P, NB * NT, E], F32)
        V = sb("V", [P, NT, KV, VW], F32)
        KS = sb("KS", [R + 1, KV, S], F32R)
        QS = sb("QS", [R + 1, 4, 4, S], F32R)
        PT = sb("PT", [P, 2, 8 * BANK], F32)
        Z = sb("Z", [P, NT, D], F32)
        negm = sb("negm", [P, 4, NT], F32)
        mT = sb("mT", [4 * NT, P], F32R)
        OS = sb("OS", [P, S], F32)
        rden = sb("rden", [P, NT, 4, 1], F32)
        ln = ln_scratch(sb, "x0_ln")
        M = [ps(f"M{i}", [P, 2 * BANK]) for i in range(2)]
        T = ps("T", [P, 2 * BANK])
        O = [ps(f"O{i}", [P, BANK]) for i in range(2)]

        tok_in, v_made, ones_set = sem("tok_in"), sem("v_made"), sem("ones_set")
        xb_in = sem("xb_in")
        ctx_hi, ctx_lo = sem("ctx_hi"), sem("ctx_lo")
        m_full = sem("m_full")
        m_free = sem("m_free")
        hi_done = sem("hi_done")
        t_full = sem("t_full")
        t_free = sem("t_free")
        pv_full = sem("pv_full")
        o_free = sem("o_free")
        keys, late_keys = sem("keys"), sem("late_keys")
        stacked = [sem(f"stacked{i}") for i in range(4)]
        shifted = [sem("shifted0"), sem("shifted1")]
        between = sem("between")
        norm = sem("norm")

        EARLY = 6
        before = [("M", "xt", 0), ("M", "xt", 1)] + [("M", "max", (0, u)) for u in range(8)] + [("M", "mt", 0)]

        def plan_of(more):
            plan = []
            for g in range(G):
                spread, units = [2, 2, 2, 2, 0, 0, 0, 0], iter(range(8))
                for s in range(8):
                    plan.append(("S", g, s))
                    if g + 1 < G or more:
                        nxt = (g + 1) % G
                        plan += [("M", "max", (nxt, next(units))) for _ in range(spread[s])]
                        if s == 5:
                            plan.append(("M", "mt", nxt))
                    if g == 5 and s < 2 and more:
                        plan.append(("M", "xt", s))
                    q = 2 * g + s // 4 - 1
                    if s == 5 and g >= 1:
                        plan.append(("M", "turn", g - 1))
                    if q >= 0:
                        plan.append(("P", q, s % 4))
            return plan + [("P", 2 * G - 1, c) for c in range(4)] + [("M", "turn", G - 1)]

        units_of = lambda plan: [x for x in plan if x[0] == "M"]
        index_of = lambda plan: {(x[1], x[2]): n for n, x in enumerate(units_of(plan))}
        PRE, MU, SU, PU = len(before), len(units_of(plan_of(True))), 8 * G, 2 * G
        assert MU % 2 == 0
        BODY, LAST = (plan_of(True), index_of(plan_of(True))), (plan_of(False), index_of(plan_of(False)))
        early = index_of(before)

        def unit(b, at, kind, arg):
            return early[kind, arg] if b is None else b * MU + (PRE + at[kind, arg])

        def tile(b, at, kind, arg):
            return M[(early[kind, arg] if b is None else PRE + at[kind, arg]) % 2]

        def own(b, kind, arg):
            ahead = kind == "xt" or (kind == "max" and arg[0] == 0) or (kind == "mt" and arg == 0)
            return 0 if b is None else b + 1 if ahead else b

        block = ctx.enter_context(nc.Block())

        @block.sync
        def _(sp):
            sp.wait_ge(ones_set, 3)
            for b in range(NB):
                sp.dma_start(CTOK[:, NT * b:NT * (b + 1), :],
                             A["ctx_512"][b].rearrange("(i p) e -> p i e", p=P)).then_inc(tok_in, 16)

            def shift_row(b, at, g, after=None):
                sp.wait_ge(m_free, unit(after, at, "mt", g) + 3)
                sp.dma_start(QS[R:R + 1, g % 4, :, :].bitcast(F32).rearrange("p h (i q) -> p (h i) q", i=NT),
                             mT[:, :].bitcast(F32)).then_inc(shifted[g % 2], 16)

            def stack_queries(g):
                for h in range(4):
                    rows = slice(HD * (4 * (g % 2) + h), HD * (4 * (g % 2) + h + 1))
                    for n, part in enumerate((XTH, XTH, XTL)):
                        sp.dma_start(QS[HD * n:HD * (n + 1), g % 4, h, :].bitcast(F32),
                                     part[rows, g // 2, :].bitcast(F32)).then_inc(stacked[g % 4], 16)

            def stack_keys(groups):
                for j in groups:
                    rows = slice(HD * j, HD * (j + 1))
                    for n, part in enumerate((CH, CL, CH)):
                        sp.dma_start(KS[HD * n:HD * (n + 1), j, :].bitcast(F32),
                                     part[rows, :].bitcast(F32)).then_inc(keys if j < EARLY else late_keys, 16)

            def scores_done(b, groups):
                sp.sem_inc(between, 1)
                sp.wait_ge(t_full, b * SU + 8 * groups)

            def batch(b, at, more):
                stack_keys(range(EARLY, G))
                for g in (2, 3):
                    stack_queries(g)
                for g in range(1, G):
                    shift_row(b, at, g, b)
                    if g <= 4:
                        scores_done(b, g)
                        stack_queries(g + 3)
                    elif more and g == 5:
                        sp.sem_inc(between, 1)
                        sp.wait_ge(m_free, unit(b, at, "xt", 1) + 3)
                        scores_done(b, 5)
                        stack_keys(range(5))
                    elif more and g == 6:
                        stack_queries(0)
                if more:
                    scores_done(b, 6)
                    stack_queries(1)
                    stack_keys(range(5, EARLY))
                    sp.sem_inc(between, 1)
                    shift_row(b + 1, at, 0, b)
                    scores_done(b, 8)
                    sp.sem_inc(between, 1)

            sp.wait_ge(ctx_lo, 1)
            sp.wait_ge(m_free, unit(None, None, "xt", 1) + 3)
            stack_keys(range(EARLY))
            stack_queries(0)
            shift_row(0, None, 0)
            stack_queries(1)
            with sp.Fori(0, NB - 1) as b:
                batch(b, BODY[1], True)
            batch(NB - 1, LAST[1], False)

        @block.gpsimd
        def _(pool):
            pool.memset(V[:], 0.0).then_inc(ones_set, 1)
            pool.wait_ge(ones_set, 1)
            pool.memset(V[:, :, :, HD], 1.0).then_inc(ones_set, 1)
            pool.wait_ge(ones_set, 2)
            pool.memset(KS[32:R + 1, :, :].bitcast(F32), 1.0).then_inc(ones_set, 1)

            def load(b):
                pool.dma_start(XB[:], X[:, b, :, :]).then_inc(xb_in, 16)
                pool.dma_start(CB[:], A["ctxT"][b]).then_inc(xb_in, 16)

            load(0)
            pool.wait_ge(m_full, 2)
            pool.wait_ge(ctx_lo, 1)
            load(1)
            with pool.Fori(0, NB - 2) as b:
                pool.wait_ge(m_full, unit(b, BODY[1], "xt", 1) + 1)
                pool.wait_ge(ctx_lo, b + 2)
                load(b + 2)

        @block.scalar
        def _(act):
            act.wait_ge(tok_in, 16 * NB)
            act.wait_ge(ones_set, 2)
            act.sem_inc(t_free, 1)
            act.sem_inc(o_free, 2)

            def turned(b, at, half):
                n = own(b, "xt", half)
                if half == 0:
                    act.wait_ge(xb_in, n * 32 + 32)
                    if b is not None:
                        act.wait_ge(keys, n * (16 * 3 * EARLY))
                        act.wait_ge(late_keys, n * (16 * 3 * (G - EARLY)))
                    ac.activation(CH[:], CB[:], ACT.Copy).then_inc(ctx_hi, 1)
                    if b is not None:
                        for i in range(4):
                            act.wait_ge(stacked[i], n * (16 * 2 * 12))
                act.wait_ge(m_full, unit(b, at, "xt", half) + 1)
                ac.activation(XTH[:, 2 * half:2 * half + 2, :].rearrange("p k s -> p (k s)"), tile(b, at, "xt", half)[:],
                              ACT.Identity).then_inc(hi_done, 1)

            def batch(b, plan, at):
                act.wait_ge(pv_full, b * PU)
                act.sem_inc(between, 1)
                ac.activation(V[:, :, :, 0:HD], CTOK[:, bass.ds(b * NT, NT), :].rearrange("p t (h d) -> p t h d", h=KV),
                              ACT.Copy).then_inc(v_made, 1)
                for x in plan:
                    if x[0] == "M" and x[1] == "xt":
                        turned(b, at, x[2])
                    elif x[0] == "S":
                        g, s = x[1:]
                        pair = 2 * g + s // 4
                        act.wait_ge(t_full, b * SU + 8 * g + s + 1)
                        if s % 4 == 0 and pair >= 2:
                            act.wait_ge(pv_full, b * PU + pair - 1)
                        ac.activation(PT[:, pair % 2, 1024 * (s % 4):1024 * (s % 4 + 1)], T[:],
                                      ACT.Exp, scale=SCALE).then_inc(t_free, 1)
                    elif x[0] == "P" and x[1] % 2 == 1 and x[2] == 3:
                        q = x[1]
                        act.wait_ge(pv_full, b * PU + q + 1)
                        if q >= 3:
                            act.wait_ge(m_full, unit(b, at, "turn", q // 2 - 1) + 1)
                        ac.activation(OS[:], O[q // 2 % 2][:], ACT.Identity).then_inc(o_free, 1)

            for half in range(2):
                turned(None, None, half)
            with act.Fori(0, NB - 1) as b:
                batch(b, *BODY)
            batch(NB - 1, *LAST)

        @block.vector
        def _(dve):
            dve.sem_inc(m_free, 2)

            def through(b, at, kind, arg, step=None):
                n = unit(b, at, kind, arg)
                m = tile(b, at, kind, arg)
                w = own(b, kind, arg)
                if (kind, arg) == ("xt", 0):
                    dve.wait_ge(ctx_hi, w + 1)
                    ve.tensor_tensor(CL[:], CB[:], CH[:].bitcast(F32), ALU.subtract).then_inc(ctx_lo, 1)
                dve.wait_ge(m_full, n + 1)
                if kind == "xt":
                    dve.wait_ge(hi_done, w * 2 + arg + 1)
                    ks = slice(2 * arg, 2 * arg + 2)
                    last = ve.tensor_tensor(XTL[:, ks, :].rearrange("p k s -> p (k s)"), m[:],
                                            XTH[:, ks, :].bitcast(F32).rearrange("p k s -> p (k s)"),
                                            ALU.subtract)
                elif kind == "max":
                    g, u = arg
                    h, i = u // 2, 2 * (u % 2)
                    last = ve.tensor_reduce(negm[:, h, i:i + 2], m[:].rearrange("p (i k) -> p i k", i=2),
                                            AX.X, ALU.max, negate=True)
                elif kind == "mt":
                    if arg >= 1:
                        dve.wait_ge(shifted[(arg - 1) % 2], (w * 4 + (arg - 1) // 2 + 1) * 16)
                    elif b is not None:
                        dve.wait_ge(shifted[(G - 1) % 2], w * (4 * 16))
                    last = ve.tensor_copy(mT[:, :], m[0:4 * NT, 0:P])
                elif kind == "turn":
                    o = m[:, 0:S].rearrange("p (i h d) -> p i h d", i=NT, h=4)
                    step(ve.reciprocal(rden[:], o[:, :, :, HD:HD + 1]))
                    for h in range(4):
                        c = HD * (4 * arg + h)
                        last = ve.tensor_tensor(Z[:, :, c:c + HD], o[:, :, h, 0:HD],
                                                rden[:, :, h].to_broadcast([P, NT, HD]), ALU.mult)
                last.then_inc(m_free, 1)
                dve.wait_ge(m_free, n + 3)

            def normalise(step, b):
                step(ve.tensor_tensor(Z[:], Z[:], X[:, b, :, :], ALU.add))
                emit_layernorm(nc, step, Z, X[:, b, :, :], ln)
                step.done()

            def parts(plan):
                units = units_of(plan)
                cut = units.index(("M", "mt", 1)) + 1
                return units[:cut], units[cut:]

            STEPS = G + 1 + LN_STEPS
            for x in before:
                through(None, None, *x[1:])
            for x in parts(BODY[0])[0]:
                through(0, BODY[1], *x[1:])
            with dve.Fori(0, NB - 1) as b:
                step = Steps(dve, norm, b, STEPS)
                for x in parts(BODY[0])[1]:
                    through(b, BODY[1], *x[1:], step)
                for x in parts(BODY[0])[0]:
                    through(b + 1, BODY[1], *x[1:])
                normalise(step, b)
            step = Steps(dve, norm, NB - 1, STEPS)
            for x in parts(LAST[0])[1]:
                through(NB - 1, LAST[1], *x[1:], step)
            normalise(step, NB - 1)

        @block.tensor
        def _(t):
            t.wait_ge(ones_set, 3)

            def fill(b, at, kind, arg):
                m = tile(b, at, kind, arg)
                w = own(b, kind, arg)
                t.wait_ge(m_free, unit(b, at, kind, arg) + 1)
                if kind == "xt":
                    if arg == 0:
                        t.wait_ge(xb_in, w * 32 + 32)
                    for k in range(2):
                        for i in range(NT):
                            c = P * (2 * arg + k)
                            last = pe.transpose(m[:, BANK * k + P * i:BANK * k + P * (i + 1)],
                                                XB[:, i, c:c + P], C["ident"][:])
                elif kind == "max":
                    g, u = arg
                    if u == 0:
                        if g == 0:
                            t.wait_ge(keys, w * (16 * 3 * EARLY) + 16 * 3 * EARLY)
                        if g == EARLY:
                            t.wait_ge(late_keys, w * (16 * 3 * (G - EARLY)) + 16 * 3 * (G - EARLY))
                        t.wait_ge(stacked[g % 4], w * (2 * 16 * 12) + (g // 4 + 1) * 16 * 12)
                    for k in range(2):
                        i = 2 * (u % 2) + k
                        last = pe.matmul(m[:, BANK * k:BANK * (k + 1)], QS[0:R, g % 4, u // 2, P * i:P * (i + 1)],
                                         KS[0:R, g, :], start=True, stop=True)
                elif kind == "mt":
                    t.wait_ge(m_free, unit(b, at, "max", (arg, 7)) + 3)
                    last = pe.transpose(m[0:4 * NT, 0:P], negm[:].rearrange("p h i -> p (h i)"), C["ident"][:])
                elif kind == "turn":
                    t.wait_ge(o_free, b * G + arg + 3)
                    for i in range(NT):
                        last = pe.transpose(m[:, P * i:P * (i + 1)], OS[:, P * i:P * (i + 1)], C["ident"][:])
                last.then_inc(m_full, 1)

            def batch(b, plan, at):
                for x in plan:
                    if x[0] == "M":
                        fill(b, at, *x[1:])
                    elif x[0] == "S":
                        g, s = x[1:]
                        if s == 0:
                            t.wait_ge(shifted[g % 2], (b * 4 + g // 2 + 1) * 16)
                        t.wait_ge(t_free, b * SU + 8 * g + s + 1)
                        for k in range(2):
                            j = 2 * (s % 2) + k
                            last = pe.matmul(T[:, BANK * k:BANK * (k + 1)], KS[0:R + 1, g, P * j:P * (j + 1)],
                                             QS[0:R + 1, g % 4, s // 2, :], start=True, stop=True)
                        last.then_inc(t_full, 1)
                    else:
                        q, part = x[1:]
                        o = O[q // 2 % 2]
                        if part == 0:
                            if q == 0:
                                t.wait_ge(v_made, b + 1)
                            if q % 2 == 0:
                                t.wait_ge(o_free, b * G + q // 2 + 1)
                            t.wait_ge(t_free, b * SU + 4 * (q + 1) + 1)
                        for h, j in [(h, j) for h in range(2) for j in range(NT)][2 * part:2 * part + 2]:
                            r0 = VW * (2 * (q % 2) + h)
                            last = pe.matmul(o[r0:r0 + VW, :], V[:, j, q // 2, :],
                                             PT[:, q % 2, BANK * (NT * h + j):BANK * (NT * h + j + 1)],
                                             start=(j == 0), stop=(j == NT - 1))
                        if part == 3:
                            last.then_inc(pv_full, 1)

            for x in before:
                fill(None, None, *x[1:])
            with t.Fori(0, NB - 1) as b:
                batch(b, *BODY)
            batch(NB - 1, *LAST)


def stage_ffn(nc, X, C, A):
    F = 2048
    FC = F // P
    NTILE = NB * NT
    QB, EPS = 128.0, 1e-5
    CW = F ** -0.5
    pe, ve, ac, gp = nc.tensor, nc.vector, nc.scalar, nc.gpsimd
    ctx = ExitStack()
    with ctx:
        sb = lambda n, s, d: ctx.enter_context(nc.sbuf_tensor(f"ffn_{n}", s, d))
        ps = lambda n, w: ctx.enter_context(nc.psum_tensor(f"ffn_{n}", [P, w], F32))
        sem = own_semaphores(nc, ctx, f"ffn")

        XF = X[:].rearrange("p b i d -> p (b i) d")
        WG = sb("WG", [P, KC, F], BF16)
        WU = sb("WU", [P, KC, F], BF16)
        WD = sb("WD", [P, FC, D], BF16)
        HM = sb("HM", [P, 4, BANK], F32R)
        XQF = sb("XQF", [P, D], F32)
        XQ = sb("XQ", [P, D], BF16)
        XQT = sb("XQT", [P, KC, P], BF16)
        SG = sb("SG", [P, 2, BANK], F32)
        YQ = sb("YQ", [P, F], BF16)
        YQT = sb("YQT", [P, FC, P], BF16)
        small = lambda n, w: sb(n, [P, w], F32)
        xscale, gscale, uscale = small("xscale", NTILE), small("gscale", NTILE), small("uscale", NTILE)
        xmax = small("xmax", NTILE)
        wsum, wmean, thr, nthr = small("wsum", 3), small("wmean", 3), small("thr", 3), small("nthr", 3)
        ymax, yinv, yscale, deq = small("ymax", 1), small("yinv", 1), small("yscale", 1), small("deq", 1)
        magic = small("magic", 1)
        ones = sb("ones", [P, P], F32)
        stats = sb("stats", [P, NTILE, 6], F32)
        mean, var, rstd, tmp = (small(n, NTILE) for n in ("mean", "var", "rstd", "tmp"))
        RAW = [sb(f"RAW{i}", [P, 8192], F32) for i in range(2)]
        INT = RAW[1][:, 0:F]
        Y4 = RAW[1][:, F:2 * F]
        Y = RAW[1][:, 2 * F:3 * F]
        S13 = RAW[1][:, 3 * F:3 * F + 1024]
        SIGN = RAW[1][:, 0:2048]
        ITH = sb("ITH", [P, FC, P], F32R)
        ITL = sb("ITL", [P, FC, P], F32R)

        GU = ps("GU", 2 * BANK)
        TT = ps("TT", 2 * BANK)
        R = [ps(f"R{i}", 2 * BANK) for i in range(2)]

        w_in, w_abs, w_sum, w_mean, w_cut, w_made = (sem(n) for n in ("w_in", "w_abs", "w_sum", "w_mean", "w_cut", "w_made"))
        w_in2 = sem("w_in2")
        between = sem("between")
        sign_in, sign_made, ones_set = sem("sign_in"), sem("sign_made"), sem("ones_set")
        prep = sem("prep")
        xq_done, gu_full, gu_free = sem("xq_done"), sem("gu_full"), sem("gu_free")
        silu_done = sem("silu_done")
        th_full, th_hi, th_free = sem("th_full"), sem("th_hi"), sem("th_free")
        h_full, h_copied, bf_done = sem("h_full"), sem("h_copied"), sem("bf_done")
        quant, rounded, yq_done = sem("quant"), sem("rounded"), sem("yq_done")
        yt_full, yt_free = sem("yt_full"), sem("yt_free")
        z_done, stat, norm = sem("z_done"), sem("stat"), sem("norm")
        xq1, xt_full, d_full = sem("xq1"), sem("xt_full"), sem("d_full")

        wpart = small("wpart", 12)
        QSTEPS, PREP = 7, NTILE + 3 + 15 + 2
        before_gu = lambda s: 1 + 5 * s
        HEAD, TAIL = (-1, 0, 1), (15, 16, 17)
        HALVES = (slice(0, F // 2), slice(F // 2, F))
        has = lambda s, lo, hi: not isinstance(s, int) or lo <= s <= hi

        block = ctx.enter_context(nc.Block())

        @block.sync
        def _(sp):
            srcs = [A["w_gateT"].rearrange("(k p) n -> p k n", p=P), A["w_upT"].rearrange("(k p) n -> p k n", p=P),
                    A["w_downT"].rearrange("(c p) n -> p c n", p=P)]
            for w in range(3):
                if w == 2:
                    sp.wait_ge(w_made, 1)
                dst = RAW[w % 2][:].rearrange("p (k n) -> p k n", k=srcs[w].shape[1])
                sp.dma_start(dst, srcs[w]).then_inc((w_in, w_in2, w_in)[w], 16)
            sp.wait_ge(w_made, 2)
            sp.dma_start(SIGN, A["signs"]).then_inc(sign_in, 16)

        @block.gpsimd
        def _(pool):
            pool.memset(ones[:], 1.0).then_inc(ones_set, 1)
            pool.memset(magic[:], MAGIC).then_inc(ones_set, 1)

        @block.scalar
        def _(act):
            for w in range(3):
                act.wait_ge((w_in, w_in2, w_in)[w], (16, 16, 32)[w])
                for q in range(4):
                    dst = WD[:].rearrange("p c n -> p (c n)")[:, F * q:F * (q + 1)]
                    if w or q:
                        act.wait_ge(w_abs, 4 * w + q)
                    ac.activation(dst, RAW[w % 2][:, F * q:F * (q + 1)], ACT.Abs,
                                  accum_out=wpart[:, 4 * w + q:4 * w + q + 1]).then_inc(w_abs, 1)
            act.wait_ge(sign_in, 16)
            ac.activation(HM[:].rearrange("p c n -> p (c n)"), SIGN, ACT.Copy).then_inc(sign_made, 1)
            act.wait_ge(ones_set, 2)
            act.wait_ge(prep, PREP)

            def step(s):
                if has(s, 1, 16):
                    t = s - 1
                    act.wait_ge(th_full, 2 * t + 1)
                    ac.activation(ITH[:, 0:8, :].rearrange("p c n -> p (c n)"), TT[:], ACT.Identity).then_inc(th_hi, 1)
                if has(s, 2, 17):
                    t = s - 2
                    act.wait_ge(h_full, 2 * t + 2)
                    act.wait_ge(bf_done, t)
                    ac.activation(S13[:, 0:BANK], R[0][:, BANK:], ACT.Identity)
                    ac.activation(S13[:, BANK:], R[1][:, BANK:], ACT.Identity).then_inc(h_copied, 1)
                for u in range(4):
                    if has(s, 0, 15):
                        act.wait_ge(gu_full, 4 * s + u + 1)
                        act.sem_inc(between, 1)
                        ac.activation(SG[:, u % 2, :], GU[:, 0:BANK], ACT.Silu,
                                      scale=gscale[:, bass.ds(s, 1)]).then_inc(silu_done, 1)
                    if u == 0 and has(s, 1, 16):
                        t = s - 1
                        act.wait_ge(th_full, 2 * t + 2)
                        ac.activation(ITH[:, 8:16, :].rearrange("p c n -> p (c n)"), TT[:], ACT.Identity).then_inc(th_hi, 1)
                if has(s, 2, 17):
                    t = s - 2
                    act.wait_ge(quant, QSTEPS * (t + 1))
                    for half in HALVES:
                        ac.activation(Y[:, half], Y[:, half], ACT.Identity, scale=yscale[:, 0:1],
                                      bias=magic[:, 0:1]).then_inc(rounded, 1)
                    for v, half in enumerate(HALVES):
                        act.wait_ge(yt_full, 2 * t + v + 1)
                        ac.activation(YQT[:].rearrange("p c n -> p (c n)")[:, half], TT[:].bitcast(BF16)[:, half],
                                      ACT.Copy).then_inc(yt_free, 1)

            for s in HEAD:
                step(s)
            with act.Fori(2, 15) as s:
                step(s)
            for s in TAIL:
                step(s)

        @block.vector
        def _(dve):
            pre = Steps(dve, prep, 0, PREP)
            for t in range(NTILE):
                pre(ve.tensor_reduce(xmax[:, t:t + 1], XF[:, t, :], AX.X, ALU.max, apply_absolute_value=True))
            pre(ve.tensor_scalar(xmax[:], xmax[:], EPS, None, ALU.max))
            pre(ve.reciprocal(xscale[:], xmax[:]))
            pre(ve.tensor_scalar(xscale[:], xscale[:], QB, None, ALU.mult))
            for w, (dst, kn) in enumerate(((WG, KC), (WU, KC), (WD, FC))):
                dve.wait_ge(w_abs, 4 * (w + 1))
                pre(ve.reduce_sum(wsum[:, w:w + 1], wpart[:, 4 * w:4 * w + 4], AX.X))
                dve.wait_ge(w_sum, w + 1)
                pre(ve.tensor_scalar(wmean[:, w:w + 1], R[0][:, w:w + 1], 1.0 / (D * F), EPS, ALU.mult, ALU.max))
                pre(ve.tensor_scalar(thr[:, w:w + 1], wmean[:, w:w + 1], 0.5, None, ALU.mult))
                pre(ve.tensor_scalar(nthr[:, w:w + 1], wmean[:, w:w + 1], -0.5, None, ALU.mult))
                flat = dst[:].rearrange("p k n -> p (k n)")
                pre(ve.tensor_scalar(flat, RAW[w % 2][:], thr[:, w:w + 1], None, ALU.is_gt))
                ve.scalar_tensor_tensor(out=flat, in0=RAW[w % 2][:], scalar=nthr[:, w:w + 1], in1=flat,
                                        op0=ALU.is_lt, op1=ALU.subtract).then_inc(w_made, 1)
                dve.wait_ge(w_made, w + 1)
            for w, dst in enumerate((gscale, uscale)):
                pre(ve.tensor_scalar(dst[:], xmax[:], wmean[:, w:w + 1], -1.0 / QB, ALU.mult, ALU.mult))
            pre.done()
            dve.wait_ge(sign_made, 1)

            def quantise_x(t):
                dve.wait_ge(xq_done, t)
                ve.tensor_scalar(XQF[:], XF[:, t, :], xscale[:, bass.ds(t, 1)], MAGIC, ALU.mult, ALU.add).then_inc(xq1, 1)
                dve.wait_ge(xq1, t + 1)
                ve.tensor_scalar(XQ[:], XQF[:], MAGIC, QB - 1, ALU.subtract, ALU.min).then_inc(xq_done, 1)

            def step(s):
                def lower(v):
                    t = s - 1
                    dve.wait_ge(th_hi, 2 * t + v + 1)
                    cs = slice(8 * v, 8 * v + 8)
                    ve.tensor_tensor(ITL[:, cs, :].rearrange("p c n -> p (c n)"), TT[:],
                                     ITH[:, cs, :].bitcast(F32).rearrange("p c n -> p (c n)"),
                                     ALU.subtract).then_inc(th_free, 1)

                def gate_up(u):
                    dve.wait_ge(silu_done, 4 * s + u + 1)
                    if not isinstance(s, int) or s >= 1:
                        dve.wait_ge(th_full, 2 * (s - 1) + (1 if u < 2 else 2))
                    ve.scalar_tensor_tensor(out=INT[:, BANK * u:BANK * (u + 1)], in0=GU[:, BANK:],
                                            scalar=uscale[:, bass.ds(s, 1)], in1=SG[:, u % 2, :],
                                            op0=ALU.mult, op1=ALU.mult).then_inc(gu_free, 1)

                def butterfly():
                    t = s - 2
                    dve.wait_ge(h_copied, t + 1)
                    for i in range(2):
                        for j, op in enumerate((ALU.add, ALU.subtract)):
                            last = ve.tensor_tensor(Y4[:, BANK * (2 * i + j):BANK * (2 * i + j + 1)], R[i][:, 0:BANK],
                                                    S13[:, BANK * i:BANK * (i + 1)], op)
                    last.then_inc(bf_done, 1)
                    dve.wait_ge(bf_done, t + 1)

                if has(s, 2, 17):
                    q = Steps(dve, quant, s - 2, QSTEPS)
                if has(s, 1, 16):
                    lower(0)
                if has(s, 0, 15):
                    gate_up(0)
                if has(s, 2, 17):
                    butterfly()
                if has(s, 1, 16):
                    lower(1)
                if has(s, 0, 15):
                    gate_up(1)
                if has(s, 2, 17):
                    dve.wait_ge(yq_done, 2 * s - 4)
                    q(ve.tensor_tensor(Y[:, 0:1024], Y4[:, 0:1024], Y4[:, 1024:], ALU.add))
                    q(ve.tensor_tensor(Y[:, 1024:], Y4[:, 0:1024], Y4[:, 1024:], ALU.subtract))
                if has(s, 0, 15):
                    gate_up(2)
                if has(s, 2, 17):
                    q(ve.tensor_reduce(ymax[:], Y, AX.X, ALU.max, apply_absolute_value=True))
                    q(ve.tensor_scalar(ymax[:], ymax[:], CW, EPS, ALU.mult, ALU.max))
                    q(ve.reciprocal(yinv[:], ymax[:]))
                    q(ve.tensor_scalar(yscale[:], yinv[:], QB * CW, None, ALU.mult))
                    q(ve.tensor_scalar(deq[:], ymax[:], wmean[:, 2:3], -1.0 / QB, ALU.mult, ALU.mult))
                    q.done()
                if has(s, -1, 14):
                    if not isinstance(s, int) or s >= 0:
                        dve.wait_ge(xt_full, s + 1)
                    quantise_x(s + 1)
                if has(s, 0, 15):
                    gate_up(3)
                if has(s, 2, 17):
                    dve.wait_ge(yt_full, 2 * s - 4)
                    for v, half in enumerate(HALVES):
                        dve.wait_ge(rounded, 2 * s - 3 + v)
                        ve.tensor_scalar(YQ[:, half], Y[:, half], MAGIC, QB - 1, ALU.subtract, ALU.min).then_inc(yq_done, 1)
                if isinstance(s, int) and s >= 16:
                    n = before_gu(16) + (s - 16)
                elif isinstance(s, int) and s == -1:
                    n = 0
                else:
                    n = before_gu(s) + 4
                if has(s, -1, 14):
                    dve.wait_ge(xt_full, s + 2)
                    inst = ve.tensor_copy(XQT[:].rearrange("p k n -> p (k n)"), GU[:, BANK:BANK + 256].bitcast(BF16))
                    if not has(s, 2, 17):
                        inst.then_inc(gu_free, 1)
                if has(s, 2, 17):
                    t = s - 2
                    dve.wait_ge(d_full, t + 1)
                    ve.scalar_tensor_tensor(out=XF[:, t, :], in0=GU[:, 0:BANK], scalar=deq[:, 0:1],
                                            in1=XF[:, t, :], op0=ALU.mult, op1=ALU.add).then_inc(gu_free, 1)
                    dve.wait_ge(gu_free, n + 1)
                    ve.bn_stats(stats[:, t, :], XF[:, t, :]).then_inc(stat, 1)

            for s in HEAD:
                step(s)
            with dve.Fori(2, 15) as s:
                step(s)
            for s in TAIL:
                step(s)
            dve.wait_ge(stat, NTILE)
            fin = Steps(dve, norm, 0, RSTD_STEPS + NTILE)
            emit_rstd(nc, fin, stats[:], mean[:], var[:], rstd[:], tmp[:])
            for t in range(NTILE):
                fin(ve.tensor_scalar(XF[:, t, :], XF[:, t, :], mean[:, t:t + 1], rstd[:, t:t + 1],
                                     ALU.subtract, ALU.mult))
            fin.done()

        @block.tensor
        def _(t_):
            eng = t_
            eng.wait_ge(ones_set, 2)
            for w in range(3):
                eng.wait_ge(prep, NTILE + 3 + 5 * w + 1)
                pe.matmul(R[0][:, w:w + 1], ones[:], wsum[:, w:w + 1], start=True, stop=True).then_inc(w_sum, 1)
            eng.wait_ge(prep, PREP)
            eng.wait_ge(sign_made, 1)

            def turn_half(s, v):
                t = s - 1
                if v == 0:
                    if not isinstance(s, int) or s > 1:
                        eng.wait_ge(yt_free, 2 * t - 2)
                    eng.wait_ge(gu_free, before_gu(t) + 4)
                else:
                    eng.wait_ge(th_free, 2 * t + 1)
                for c in range(8):
                    f = P * (8 * v + c)
                    last = pe.transpose(TT[:, P * c:P * (c + 1)], INT[:, f:f + P], C["ident"][:])
                last.then_inc(th_full, 1)

            def gate_up(s, u):
                eng.wait_ge(gu_free, before_gu(s) + u)
                for w, W in enumerate((WG, WU)):
                    for k in range(KC):
                        last = pe.matmul(GU[:, BANK * w:BANK * (w + 1)], XQT[:, k, :], W[:, k, BANK * u:BANK * (u + 1)],
                                         start=(k == 0), stop=(k == KC - 1))
                last.then_inc(gu_full, 1)

            def transform(s, v):
                t = s - 1
                if v == 0:
                    eng.wait_ge(bf_done, t)
                eng.wait_ge(th_free, 2 * t + v + 1)
                for j in range(2):
                    n = 0
                    for c in range(4):
                        for part in (ITH, ITL):
                            last = pe.matmul(R[v][:, BANK * j:BANK * (j + 1)], part[:, 4 * (2 * v + j) + c, :],
                                             HM[:, c, :], start=(n == 0), stop=(n == 7))
                            n += 1
                last.then_inc(h_full, 1)

            def step(s):
                if has(s, 1, 16):
                    turn_half(s, 0)
                if has(s, 0, 15):
                    gate_up(s, 0)
                if has(s, 1, 16):
                    turn_half(s, 1)
                if has(s, 0, 15):
                    gate_up(s, 1)
                if has(s, 1, 16):
                    transform(s, 0)
                if has(s, 0, 15):
                    gate_up(s, 2)
                if has(s, 1, 16):
                    transform(s, 1)
                if has(s, 0, 15):
                    gate_up(s, 3)
                if has(s, -1, 14):
                    eng.wait_ge(gu_free, 0 if isinstance(s, int) and s == -1 else before_gu(s) + 4)
                    eng.wait_ge(xq_done, s + 2)
                    for k in range(KC):
                        last = pe.transpose(GU[:, BANK:BANK + 256].bitcast(BF16)[:, P * k:P * (k + 1)],
                                            XQ[:, P * k:P * (k + 1)], C["identb"][:])
                    last.then_inc(xt_full, 1)
                if has(s, 2, 17):
                    t = s - 2
                    eng.wait_ge(th_free, 2 * NTILE if isinstance(s, int) and s == 17 else 2 * s)
                    for v in range(2):
                        eng.wait_ge(yq_done, 2 * t + v + 1)
                        for c in range(v * FC // 2, (v + 1) * FC // 2):
                            last = pe.transpose(TT[:].bitcast(BF16)[:, P * c:P * (c + 1)], YQ[:, P * c:P * (c + 1)],
                                                C["identb"][:])
                        last.then_inc(yt_full, 1)
                    if isinstance(s, int) and s >= 15:
                        eng.wait_ge(gu_free, before_gu(15) + 4 + (s - 15))
                    for c in range(FC):
                        if c % (FC // 2) == 0:
                            eng.wait_ge(yt_free, 2 * t + 1 + (1 if c else 0))
                        last = pe.matmul(GU[:, 0:BANK], YQT[:, c, :], WD[:, c, :], start=(c == 0), stop=(c == FC - 1))
                    last.then_inc(d_full, 1)

            for s in HEAD:
                step(s)
            with eng.Fori(2, 15) as s:
                step(s)
            for s in TAIL:
                step(s)


def stage_graph(nc, X, C, A):
    E, TOPK, HALVINGS = 128, 153, 25
    NTILE = NB * NT
    DVE_TILES = 8
    SCALE = 1.0 / (32 ** 0.5 * 4)
    pe, ve, ac, gp = nc.tensor, nc.vector, nc.scalar, nc.gpsimd
    ctx = ExitStack()
    with ctx:
        sb = lambda n, s, d: ctx.enter_context(nc.sbuf_tensor(f"graph_{n}", s, d))
        ps = lambda n, w: ctx.enter_context(nc.psum_tensor(f"graph_{n}", [P, w], F32))
        sem = own_semaphores(nc, ctx, f"graph")
        XF = X[:].rearrange("p b i d -> p (b i) d")
        small = lambda n, w: sb(n, [P, w], F32)
        WQK = sb("WQK", [P, 2, E], F32)
        CT = sb("CT", [P, NB, S], F32)
        QK = sb("QK", [P, 2, S], F32)
        SIM = sb("SIM", [P, NTILE, S], F32)
        SIGM = sb("SIGM", [P, NT, S], F32)
        L = sb("L", [P, NT, S], F32)
        SUM = sb("SUM", [P, NT, S], F32)
        XS = sb("XS", [P, NT, S], F32)
        seen_v = sb("seen_v", [P, DVE_TILES, S], BF16)
        seen_a = sb("seen_a", [P, NTILE - DVE_TILES, S], BF16)
        graw, gamma, g2, gh = (small(n, 1) for n in ("graw", "gamma", "g2", "gh"))
        low, width, mid, count, take = (small(n, NTILE) for n in ("low", "width", "mid", "count", "take"))
        stats = sb("stats", [P, NTILE, 6], F32)
        mean, var, rstd, tmp = (small(n, NTILE) for n in ("mean", "var", "rstd", "tmp"))
        PP = [ps(f"P{i}", 2 * BANK) for i in range(4)]

        names = ("loaded qk_full qk_taken sim_full sim_taken ranged mid_done counted_v counted_a gam gam2 "
                 "sigm xs masked turned summed spread halved z_done stat norm between")
        q = {n: sem(n) for n in names.split()}
        block = ctx.enter_context(nc.Block())

        @block.sync
        def _(sp):
            sp.dma_start(CT[:], A["ctxT"].rearrange("b e s -> e b s")).then_inc(q["loaded"], 16)
            sp.dma_start(WQK[:], A["graph_w"]).then_inc(q["loaded"], 16)
            sp.dma_start(graw[:], A["gamma"]).then_inc(q["loaded"], 16)

        @block.tensor
        def _(t):
            t.wait_ge(q["loaded"], 48)
            with t.Fori(0, NB) as b:
                t.wait_ge(q["qk_taken"], b)
                for w in range(2):
                    last = pe.matmul(PP[0][:, BANK * w:BANK * (w + 1)], WQK[:, w, :], CT[:, b, :],
                                     start=True, stop=True)
                last.then_inc(q["qk_full"], 1)
                t.wait_ge(q["qk_taken"], b + 1)
                for v in range(2):
                    t.wait_ge(q["sim_taken"], b * 2 + v)
                    for j in range(2):
                        i = 2 * v + j
                        last = pe.matmul(PP[1 + v][:, BANK * j:BANK * (j + 1)], QK[:, 0, P * i:P * (i + 1)],
                                         QK[:, 1, :], start=True, stop=True)
                    last.then_inc(q["sim_full"], 1)
            with t.Fori(0, NB) as b:
                t.wait_ge(q["masked"], b * NT + NT)
                for v in range(2):
                    t.wait_ge(q["summed"], b * 2 + v)
                    for j in range(2):
                        i = 2 * v + j
                        for m in range(NT):
                            last = pe.transpose(PP[2 * v][:, BANK * j + P * m:BANK * j + P * (m + 1)],
                                                L[:, m, P * i:P * (i + 1)], C["ident"][:])
                    last.then_inc(q["turned"], 1)

        @block.scalar
        def _(act):
            act.wait_ge(q["loaded"], 48)
            ac.activation(gamma[:], graw[:], ACT.Sigmoid).then_inc(q["gam"], 1)
            with act.Fori(0, NB) as b:
                act.wait_ge(q["qk_full"], b + 1)
                act.wait_ge(q["sim_full"], b * 2)
                ac.activation(QK[:].rearrange("p w s -> p (w s)"), PP[0][:], ACT.Copy).then_inc(q["qk_taken"], 1)
                for v in range(2):
                    act.wait_ge(q["sim_full"], b * 2 + v + 1)
                    act.sem_inc(q["between"], 1)
                    ac.activation(SIM[:, bass.ds(b * NT + 2 * v, 2), :].rearrange("p i s -> p (i s)"), PP[1 + v][:],
                                  ACT.Copy, scale=SCALE).then_inc(q["sim_taken"], 1)
            with act.Fori(0, HALVINGS) as n:
                act.wait_ge(q["mid_done"], n + 1)
                for t in range(DVE_TILES, NTILE):
                    inst = ac.activation(seen_a[:, t - DVE_TILES, :], SIM[:, t, :], ACT.Sign, scale=-1.0,
                                         bias=mid[:, t:t + 1], accum_out=count[:, t:t + 1])
                inst.then_inc(q["counted_a"], 1)
            act.wait_ge(q["gam2"], 2)
            with act.Fori(0, NB) as b:
                act.wait_ge(q["masked"], b * NT)
                act.sem_inc(q["between"], 1)
                for i in range(NT):
                    ac.activation(SIGM[:, i, :], SIM[:, b * NT + i, :], ACT.Sigmoid).then_inc(q["sigm"], 1)
                act.wait_ge(q["z_done"], b * NT)
                act.sem_inc(q["between"], 1)
                for i in range(NT):
                    ac.activation(XS[:, i, :], XF[:, b * NT + i, :], ACT.Identity, scale=g2[:, 0:1]).then_inc(q["xs"], 1)

        @block.vector
        def _(dve):
            dve.wait_ge(q["gam"], 1)
            pre = Steps(dve, q["gam2"], 0, 2)
            pre(ve.tensor_scalar(g2[:], gamma[:], -1.0, 2.0, ALU.mult, ALU.add))
            pre(ve.tensor_scalar(gh[:], gamma[:], 0.5, None, ALU.mult))
            with dve.Fori(0, NB) as b:
                r = Steps(dve, q["ranged"], b, 4)
                for v in range(2):
                    dve.wait_ge(q["sim_taken"], b * 2 + v + 1)
                    sim = SIM[:, bass.ds(b * NT + 2 * v, 2), :]
                    r(ve.tensor_reduce(low[:, bass.ds(b * NT + 2 * v, 2)], sim, AX.X, ALU.min))
                    r(ve.tensor_reduce(width[:, bass.ds(b * NT + 2 * v, 2)], sim, AX.X, ALU.max))
            first = Steps(dve, q["spread"], 0, 2)
            first(ve.tensor_tensor(width[:], width[:], low[:], ALU.subtract))
            first(ve.tensor_scalar(width[:], width[:], 0.5, None, ALU.mult))
            with dve.Fori(0, HALVINGS) as n:
                k = Steps(dve, q["halved"], n, 4)
                ve.tensor_tensor(mid[:], low[:], width[:], ALU.add).then_inc(q["mid_done"], 1)
                dve.wait_ge(q["mid_done"], n + 1)
                for t in range(DVE_TILES):
                    inst = ve.tensor_scalar(seen_v[:, t, :], SIM[:, t, :], mid[:, t:t + 1], 0.0, ALU.is_ge, ALU.add,
                                            accum_out=count[:, t:t + 1])
                inst.then_inc(q["counted_v"], 1)
                dve.wait_ge(q["counted_v"], n + 1)
                k(ve.scalar_tensor_tensor(out=take[:, 0:DVE_TILES], in0=count[:, 0:DVE_TILES], scalar=TOPK - 0.5,
                                          in1=width[:, 0:DVE_TILES], op0=ALU.is_ge, op1=ALU.mult))
                dve.wait_ge(q["counted_a"], n + 1)
                k(ve.scalar_tensor_tensor(out=take[:, DVE_TILES:], in0=count[:, DVE_TILES:],
                                          scalar=S + 1.5 - 2 * TOPK, in1=width[:, DVE_TILES:],
                                          op0=ALU.is_le, op1=ALU.mult))
                k(ve.tensor_tensor(low[:], low[:], take[:], ALU.add))
                k(ve.tensor_scalar(width[:], width[:], 0.5, None, ALU.mult))
                k.done()
            with dve.Fori(0, NB) as b:
                dve.wait_ge(q["turned"], b * 2)
                for i in range(NT):
                    dve.wait_ge(q["sigm"], b * NT + i + 1)
                    ve.scalar_tensor_tensor(out=L[:, i, :], in0=SIM[:, b * NT + i, :], scalar=low[:, bass.ds(b * NT + i, 1)],
                                            in1=SIGM[:, i, :], op0=ALU.is_ge, op1=ALU.mult).then_inc(q["masked"], 1)
                for v in range(2):
                    dve.wait_ge(q["turned"], b * 2 + v + 1)
                    dve.wait_ge(q["masked"], b * NT + NT)
                    if v == 0:
                        dve.wait_ge(q["z_done"], b * NT)
                    ve.tensor_tensor(SUM[:, 2 * v:2 * v + 2, :].rearrange("p i s -> p (i s)"), PP[2 * v][:],
                                     L[:, 2 * v:2 * v + 2, :].rearrange("p i s -> p (i s)"), ALU.add).then_inc(q["summed"], 1)
                    dve.wait_ge(q["summed"], b * 2 + v + 1)
                    for j in range(2):
                        i = 2 * v + j
                        dve.wait_ge(q["xs"], b * NT + i + 1)
                        ve.scalar_tensor_tensor(out=XF[:, b * NT + i, :], in0=SUM[:, i, :], scalar=gh[:, 0:1],
                                                in1=XS[:, i, :], op0=ALU.mult, op1=ALU.add).then_inc(q["z_done"], 1)
                        dve.wait_ge(q["z_done"], b * NT + i + 1)
                        ve.bn_stats(stats[:, b * NT + i, :], XF[:, b * NT + i, :]).then_inc(q["stat"], 1)
            dve.wait_ge(q["stat"], NTILE)
            fin = Steps(dve, q["norm"], 0, RSTD_STEPS + NTILE)
            emit_rstd(nc, fin, stats[:], mean[:], var[:], rstd[:], tmp[:])
            for t in range(NTILE):
                fin(ve.tensor_scalar(XF[:, t, :], XF[:, t, :], mean[:, t:t + 1], rstd[:, t:t + 1],
                                     ALU.subtract, ALU.mult))
            fin.done()


def stage_experts(nc, X, C, A):
    NE, F, NTILE = 16, 256, NB * NT
    SLOT_TILES = 2 * NTILE + NE
    ctx = ExitStack()
    with ctx:
        T = {}
        def keep(n, shape, dtype):
            T[n] = ctx.enter_context(nc.sbuf_tensor(f"moe_{n}", shape, dtype))
        keep("share", [P, 2, NTILE], F32)
        keep("slot", [P, 2, NTILE], U32)
        keep("slot_token", [P, SLOT_TILES], U32)
        keep("weight_row", [P, SLOT_TILES], U32)
        dram = lambda n, shape, dt: nc.dram_tensor(f"moe_{n}", shape, dt, kind="Internal").ap()
        T["x_rows"] = dram("x_rows", (NTILE * P, D), F32)
        T["y_rows"] = dram("y_rows", (SLOT_TILES * P, D), F32)
        T["table"] = dram("table", (P * SLOT_TILES, 1), U32)
        route_and_share(nc, X, C, A, T, NE, F, SLOT_TILES)
        run_slots(nc, X, C, A, T, F, SLOT_TILES)
        combine_slots(nc, X, T)


def route_and_share(nc, X, C, A, T, NE, F, SLOT_TILES):
    NTILE = NB * NT
    pe, ve, ac, gp = nc.tensor, nc.vector, nc.scalar, nc.gpsimd
    ctx = ExitStack()
    with ctx:
        sb = lambda n, s, d: ctx.enter_context(nc.sbuf_tensor(f"share_{n}", s, d))
        ps = lambda n, w: ctx.enter_context(nc.psum_tensor(f"share_{n}", [P, w], F32))
        sem = own_semaphores(nc, ctx, f"share")
        XF = X[:].rearrange("p b i d -> p (b i) d")
        XTH = sb("XTH", [P, KC, NTILE * P], F32R)
        XTL = sb("XTL", [P, KC, NTILE * P], F32R)
        DOWN = 2 * KC * F
        WW = DOWN + 2 * D
        RAW = sb("RAW", [P, 2, WW], F32)
        WH = sb("WH", [P, WW], F32R)
        WL = sb("WL", [P, WW], F32R)
        RW = sb("RW", [P, KC, NE], F32)
        RWH = sb("RWH", [P, KC, NE], F32R)
        RWL = sb("RWL", [P, KC, NE], F32R)
        RB = sb("RB", [P, NTILE, NE], F32)
        SU = sb("SU", [P, 2, S], F32)
        H = sb("H", [P, 2, S], F32)
        HH = sb("HH", [P, 2, 2, S], F32R)
        HL = sb("HL", [P, 2, 2, S], F32R)
        routing = sb("routing", [P, 9, NTILE, NE], F32)
        LG, LB, EX, ONE0, ONE1, MASK, IOTA, SLOTS, PICK = (routing[:, i] for i in range(9))
        BEFORE = sb("BEFORE", [P, NTILE + 1, NE], F32)
        ones = sb("ones", [P, P], F32)
        earlier = sb("earlier", [P, P], F32)
        top = sb("top", [P, NTILE, 8], F32)
        idx = sb("idx", [P, NTILE, 8], U32)
        idf = sb("idf", [P, NTILE, 8], F32)
        lmax = sb("lmax", [P, NTILE, 1], F32)
        total = sb("total", [P, NTILE], F32)
        tiles_i = sb("tiles_i", [P, NE], I32)
        tiles_f = sb("tiles_f", [P, NE], F32)
        first = sb("first", [P, 1, NE + 1], F32)
        slot_f = sb("slot_f", [P, 2, NTILE], F32)
        in_tile = sb("in_tile", [P, 2, NTILE], I32)
        place_tile = sb("place_tile", [P, 2, NTILE], I32)
        place = sb("place", [P, 2, NTILE], U32)
        token_id = sb("token_id", [P, NTILE], U32)
        tile_no = sb("tile_no", [P, SLOT_TILES], F32)
        expert_f = sb("expert_f", [P, SLOT_TILES], F32)
        row = sb("row", [P, 1], F32)
        zero = sb("zero", [P, SLOT_TILES], U32)
        UG = [ps(f"UG{i}", 2 * BANK) for i in range(2)]
        Y = [ps(f"Y{i}", 2 * BANK) for i in range(2)]

        q = {n: sem(n) for n in ("router_in router_hi router_lo xt_full xt_hi xt_lo logits routed ex_done made "
                                 "counted copied zeroed scattered table_in "
                                 "w_in w_hi w_lo ug_full silu_done ug_free h_hi h_lo y_full y_free between").split()}
        UG0, H0, Y0, DONE0 = 2, 2, 4, 1
        SORTED = 4 + 2 * NTILE + 8
        ROUTE = SORTED + 5 + NTILE + 3 + NE + 10 + NE + 2
        block = ctx.enter_context(nc.Block())

        @block.sync
        def _(sp):
            sp.dma_start(RW[:], A["router_wT"].rearrange("(k p) e -> p k e", p=P)).then_inc(q["router_in"], 16)
            sp.dma_start(RB[:], A["router_b"]).then_inc(q["router_in"], 16)
            for j in range(2):
                sp.dma_start(RAW[:, j, :], A["experts"][NE + j]).then_inc(q["w_in"], 16)
            sp.dma_start(T["x_rows"].rearrange("(t p) d -> p t d", p=P), XF).then_inc(q["copied"], 16)
            sp.wait_ge(q["made"], 8)
            sp.dma_start(T["table"].rearrange("(p t) o -> p (t o)", p=P), zero[:]).then_inc(q["zeroed"], 16)
            sp.wait_ge(q["copied"], 16)
            sp.wait_ge(q["scattered"], 16 * 2 * NTILE)
            sp.dma_start(T["slot_token"][:], T["table"].rearrange("(p t) o -> p (t o)", p=P)).then_inc(q["table_in"], 16)
            sp.wait_ge(q["table_in"], 16)

        @block.gpsimd
        def _(pool):
            IMP = dict(allow_small_or_imprecise_dtypes=True)
            pool.iota(IOTA[:], pattern=[[0, NTILE], [1, NE]], base=0, channel_multiplier=0, **IMP).then_inc(q["made"], 1)
            pool.iota(token_id[:], pattern=[[P, NTILE]], base=0, channel_multiplier=1).then_inc(q["made"], 1)
            pool.iota(tile_no[:], pattern=[[1, SLOT_TILES]], base=0, channel_multiplier=0, **IMP).then_inc(q["made"], 1)
            pool.iota(row[:], pattern=[[0, 1]], base=0, channel_multiplier=1, **IMP).then_inc(q["made"], 1)
            pool.memset(ones[:], 1.0).then_inc(q["made"], 1)
            pool.memset(first[:], 0.0).then_inc(q["made"], 1)
            pool.memset(zero[:], 0).then_inc(q["made"], 1)
            pool.wait_ge(q["made"], 7)
            pool.affine_select(out=earlier[:], in_=ones[:], compare_op=ALU.is_gt, fill=0.0,
                               base=0, pattern=[[1, P]], channel_multiplier=-1).then_inc(q["made"], 1)
            pool.wait_ge(q["made"], 8)
            pool.wait_ge(q["zeroed"], 16)
            pool.wait_ge(q["routed"], ROUTE)
            for t in range(NTILE):
                for k in range(2):
                    pool.indirect_dma_start(out=T["table"], out_offset=bass.IndirectOffsetOnAxis(place[:, k, t:t + 1], 0),
                                            in_=token_id[:, t:t + 1], in_offset=None).then_inc(q["scattered"], 16)
            pool.wait_ge(q["scattered"], 16 * 2 * NTILE)

        @block.scalar
        def _(act):
            act.sem_inc(q["y_full"], DONE0)
            act.wait_ge(q["router_in"], 32)
            ac.activation(RWH[:], RW[:], ACT.Copy).then_inc(q["router_hi"], 1)
            for n in range(2 * NB):
                b, kk = n // 2, n % 2
                act.wait_ge(q["xt_full"], n + 1)
                ac.activation(XTH[:, 2 * kk:2 * kk + 2, S * b:S * (b + 1)], UG[n % 2][:].rearrange("p (k s) -> p k s", k=2),
                              ACT.Copy).then_inc(q["xt_hi"], 1)
            act.wait_ge(q["routed"], 4)
            ac.activation(EX[:], EX[:], ACT.Exp).then_inc(q["ex_done"], 1)
            act.wait_ge(q["w_in"], 32)
            with act.Fori(0, 2) as j:
                act.wait_ge(q["y_full"], j * (4 * NB) + DONE0)
                act.sem_inc(q["between"], 1)
                ac.activation(WH[:], RAW[:, bass.ds(j, 1), :].rearrange("p o w -> p (o w)"), ACT.Copy).then_inc(q["w_hi"], 1)
                for m in range(NB):
                    for h in range(2):
                        act.wait_ge(q["ug_full"], j * (2 * NB) + 2 * m + h + 1)
                        ac.activation(SU[:, h, :], UG[h][:, 0:BANK], ACT.Silu).then_inc(q["silu_done"], 1)
                    for h in range(2):
                        act.wait_ge(q["ug_free"], j * (2 * NB) + 2 * m + h + 1 + UG0)
                        ac.activation(HH[:, m % 2, h, :], H[:, h, :], ACT.Copy).then_inc(q["h_hi"], 1)

        @block.vector
        def _(dve):
            dve.wait_ge(q["router_hi"], 1)
            ve.tensor_tensor(RWL[:], RW[:], RWH[:].bitcast(F32), ALU.subtract).then_inc(q["router_lo"], 1)
            for n in range(2 * NB):
                b, kk = n // 2, n % 2
                dve.wait_ge(q["xt_hi"], n + 1)
                cs = slice(S * b, S * (b + 1))
                ve.tensor_tensor(XTL[:, 2 * kk:2 * kk + 2, cs], UG[n % 2][:].rearrange("p (k s) -> p k s", k=2),
                                 XTH[:, 2 * kk:2 * kk + 2, cs].bitcast(F32), ALU.subtract).then_inc(q["xt_lo"], 1)
            dve.wait_ge(q["logits"], 1)
            route = Steps(dve, q["routed"], 0, ROUTE)
            wide3 = lambda ap: ap[:, 0:NTILE * NE].rearrange("p (t e) -> p t e", e=NE)
            spread = lambda col: col.to_broadcast([P, NTILE, NE])
            route(ve.tensor_tensor(LB[:], wide3(Y[0]), RB[:], ALU.add))
            route(ve.tensor_copy(LG[:], wide3(Y[0])))
            route(ve.tensor_reduce(lmax[:, :, 0], LG[:], AX.X, ALU.max))
            route(ve.tensor_tensor(EX[:], LG[:], spread(lmax[:]), ALU.subtract))
            for t in range(NTILE):
                route(ve.max(top[:, t, :], LB[:, t, :]))
                route(ve.max_index(idx[:, t, :], top[:, t, :], LB[:, t, :]))
            route(ve.tensor_copy(idf[:], idx[:]))
            dve.wait_ge(q["made"], 8)
            route(ve.tensor_tensor(ONE0[:], IOTA[:], spread(idf[:, :, 0:1]), ALU.is_equal))
            route(ve.tensor_tensor(ONE1[:], IOTA[:], spread(idf[:, :, 1:2]), ALU.is_equal))
            dve.wait_ge(q["ex_done"], 1)
            for k, one in enumerate((ONE0, ONE1)):
                route(ve.tensor_tensor(PICK[:], EX[:], one[:], ALU.mult))
                route(ve.tensor_reduce(T["share"][:, k, :], PICK[:], AX.X, ALU.add))
            route(ve.tensor_tensor(MASK[:], ONE0[:], ONE1[:], ALU.add))
            assert route.n == SORTED
            route(ve.tensor_tensor(total[:], T["share"][:, 0, :], T["share"][:, 1, :], ALU.add))
            route(ve.reciprocal(total[:], total[:]))
            for k in range(2):
                route(ve.tensor_tensor(T["share"][:, k, :], T["share"][:, k, :], total[:], ALU.mult))
            dve.wait_ge(q["counted"], 1)
            route(ve.memset(BEFORE[:, 0, :], 0.0))
            for t in range(NTILE):
                route(ve.tensor_tensor(BEFORE[:, t + 1, :], BEFORE[:, t, :], wide3(Y[1][:, BANK:])[:, t, :], ALU.add))
            route(ve.tensor_scalar(tiles_i[:], BEFORE[:, NTILE, :], P - 1.0, None, ALU.add))
            route(ve.tensor_scalar(tiles_i[:], tiles_i[:], 7, None, ALU.arith_shift_right))
            route(ve.tensor_copy(tiles_f[:], tiles_i[:]))
            for e in range(NE):
                route(ve.tensor_tensor(first[:, 0, e + 1:e + 2], first[:, 0, e:e + 1], tiles_f[:, e:e + 1], ALU.add))
            route(ve.tensor_tensor(SLOTS[:], BEFORE[:, 0:NTILE, :], wide3(Y[1]), ALU.add))
            route(ve.scalar_tensor_tensor(out=SLOTS[:], in0=first[:, :, 0:NE].to_broadcast([P, NTILE, NE]),
                                          scalar=float(P), in1=SLOTS[:], op0=ALU.mult, op1=ALU.add))
            for k, one in enumerate((ONE0, ONE1)):
                route(ve.tensor_tensor(PICK[:], SLOTS[:], one[:], ALU.mult))
                route(ve.tensor_reduce(slot_f[:, k, :], PICK[:], AX.X, ALU.add))
            route(ve.tensor_copy(T["slot"][:], slot_f[:]))
            route(ve.tensor_scalar(in_tile[:], T["slot"][:].bitcast(I32), P - 1, None, ALU.bitwise_and))
            route(ve.tensor_scalar(place_tile[:], T["slot"][:].bitcast(I32), 7, None, ALU.arith_shift_right))
            route(ve.scalar_tensor_tensor(out=place[:], in0=in_tile[:], scalar=float(SLOT_TILES), in1=place_tile[:],
                                          op0=ALU.mult, op1=ALU.add))
            route(ve.memset(expert_f[:], 0.0))
            for e in range(1, NE):
                route(ve.scalar_tensor_tensor(out=expert_f[:], in0=tile_no[:], scalar=first[:, 0, e:e + 1],
                                              in1=expert_f[:], op0=ALU.is_ge, op1=ALU.add))
            route(ve.tensor_scalar(expert_f[:], expert_f[:], float(P), row[:, 0:1], ALU.mult, ALU.add))
            route(ve.tensor_copy(T["weight_row"][:], expert_f[:]))
            route.done()
            dve.sem_inc(q["ug_free"], UG0)
            dve.sem_inc(q["h_lo"], H0)
            dve.sem_inc(q["y_free"], Y0)

            def gather(j, m):
                for i in range(NT):
                    dve.wait_ge(q["y_full"], j * (4 * NB) + 4 * m + i + 1 + DONE0)
                    ve.tensor_tensor(XF[:, m * NT + i, :], Y[i // 2][:, BANK * (i % 2):BANK * (i % 2 + 1)],
                                     XF[:, m * NT + i, :], ALU.add).then_inc(q["y_free"], 1)

            dve.wait_ge(q["copied"], 16)
            with dve.Fori(0, 2) as j:
                dve.wait_ge(q["w_hi"], j + 1)
                ve.tensor_tensor(WL[:], RAW[:, bass.ds(j, 1), :].rearrange("p o w -> p (o w)"), WH[:].bitcast(F32),
                                 ALU.subtract).then_inc(q["w_lo"], 1)
                for m in range(NB):
                    for h in range(2):
                        u = 2 * m + h
                        dve.wait_ge(q["silu_done"], j * (2 * NB) + u + 1)
                        dve.wait_ge(q["h_lo"], j * (2 * NB) + u - 1 + H0)
                        ve.tensor_tensor(H[:, h, :], SU[:, h, :], UG[h][:, BANK:], ALU.mult).then_inc(q["ug_free"], 1)
                    for h in range(2):
                        u = 2 * m + h
                        dve.wait_ge(q["h_hi"], j * (2 * NB) + u + 1)
                        ve.tensor_tensor(HL[:, m % 2, h, :], H[:, h, :], HH[:, m % 2, h, :].bitcast(F32),
                                         ALU.subtract).then_inc(q["h_lo"], 1)
                    if m > 0:
                        gather(j, m - 1)
                gather(j, NB - 1)

        @block.tensor
        def _(t_):
            for n in range(2 * NB):
                b, kk = n // 2, n % 2
                if n >= 2:
                    t_.wait_ge(q["xt_lo"], n - 1)
                for k in range(2):
                    for i in range(NT):
                        f = P * (2 * kk + k)
                        last = pe.transpose(UG[n % 2][:, BANK * k + P * i:BANK * k + P * (i + 1)],
                                            XF[:, b * NT + i, f:f + P], C["ident"][:])
                last.then_inc(q["xt_full"], 1)
            t_.wait_ge(q["router_lo"], 1)
            t_.wait_ge(q["xt_lo"], 2 * NB)
            for t in range(NTILE):
                n = 0
                for xp, wp in ((XTH, RWL), (XTL, RWH), (XTH, RWH)):
                    for k in range(KC):
                        last = pe.matmul(Y[0][:, NE * t:NE * (t + 1)], xp[:, k, P * t:P * (t + 1)], wp[:, k, :],
                                         start=(n == 0), stop=(n == 3 * KC - 1))
                        n += 1
            last.then_inc(q["logits"], 1)
            t_.wait_ge(q["made"], 8)
            t_.wait_ge(q["routed"], SORTED)
            mask = MASK[:].rearrange("p t e -> p (t e)")
            pe.matmul(Y[1][:, 0:NTILE * NE], earlier[:], mask, start=True, stop=True)
            pe.matmul(Y[1][:, BANK:BANK + NTILE * NE], ones[:], mask, start=True, stop=True).then_inc(q["counted"], 1)

            def up_gate(j, m):
                for h in range(2):
                    t_.wait_ge(q["ug_free"], j * (2 * NB) + 2 * m + h - 1 + UG0)
                    for w in range(2):
                        n = 0
                        for wp, xp in ((WH, XTH), (WH, XTL), (WL, XTH)):
                            for k in range(KC):
                                c = 2 * F * k + F * w + P * h
                                last = pe.matmul(UG[h][:, BANK * w:BANK * (w + 1)], wp[:, c:c + P],
                                                 xp[:, k, S * m:S * (m + 1)], start=(n == 0), stop=(n == 3 * KC - 1))
                                n += 1
                    last.then_inc(q["ug_full"], 1)

            def down(j, m):
                t_.wait_ge(q["h_lo"], j * (2 * NB) + 2 * m + 2 + H0)
                for i in range(NT):
                    if i % 2 == 0:
                        t_.wait_ge(q["y_free"], j * (4 * NB) + 4 * m + i - 2 + Y0)
                    n = 0
                    for hp, wp in ((HH, WL), (HL, WH), (HH, WH)):
                        for h in range(2):
                            last = pe.matmul(Y[i // 2][:, BANK * (i % 2):BANK * (i % 2 + 1)],
                                             hp[:, m % 2, h, P * i:P * (i + 1)],
                                             wp[:, DOWN + D * h:DOWN + D * (h + 1)], start=(n == 0), stop=(n == 5))
                            n += 1
                    last.then_inc(q["y_full"], 1)

            t_.wait_ge(q["routed"], ROUTE)
            with t_.Fori(0, 2) as j:
                t_.wait_ge(q["w_lo"], j + 1)
                for m in range(NB):
                    up_gate(j, m)
                    if m > 0:
                        down(j, m - 1)
                down(j, NB - 1)


def run_slots(nc, X, C, A, T, F, SLOT_TILES):
    RING = 4
    TURNS = SLOT_TILES // RING
    UGW, DW = KC * 2 * F, 2 * D
    pe, ve, ac, gp = nc.tensor, nc.vector, nc.scalar, nc.gpsimd
    ctx = ExitStack()
    with ctx:
        sb = lambda n, s, d: ctx.enter_context(nc.sbuf_tensor(f"slots_{n}", s, d))
        ps = lambda n, w: ctx.enter_context(nc.psum_tensor(f"slots_{n}", [P, w], F32))
        sem = own_semaphores(nc, ctx, f"slots")

        def places(n, count, w, dtype):
            t = sb(n, [P, count, w], dtype)
            return [t[:, i, :] for i in range(count)]

        RAW = places("RAW", RING, UGW + DW, F32)
        XG = places("XG", RING, D, F32)
        YS = places("YS", RING, D, F32)
        PICK = places("PICK", RING, 2, U32)
        WH = places("WH", 2, UGW + DW, F32R)
        WL = places("WL", 2, UGW + DW, F32R)
        XTH = places("XTH", 2, KC * P, F32R)
        XTL = places("XTL", 2, KC * P, F32R)
        SU = places("SU", 2, F, F32)
        H = places("H", 2, F, F32)
        HH = sb("HH", [P, F], F32R)
        HL = sb("HL", [P, F], F32R)
        XT = ps("XT", BANK)
        U = [ps(f"U{i}", BANK) for i in range(2)]
        HT = ps("HT", BANK)
        Y = [ps(f"Y{i}", BANK) for i in range(2)]

        q = {n: sem(n) for n in ("picked xt_full x_hi x_lo up_hi down_hi up_lo up_lo_pool down_lo "
                                 "u_full silu_done h_made ht_full h_hi h_lo y_full y_taken between").split()}
        x_in, w_in, y_out = ([sem(f"{n}{i}") for i in range(RING)] for n in ("x_in", "w_in", "y_out"))
        PARTS = (slice(0, UGW // 2), slice(UGW // 2, UGW))
        DOWN = slice(UGW, UGW + DW)
        weights = A["experts"].rearrange("e p w -> (e p) w")
        block = ctx.enter_context(nc.Block())

        def run(eng, step):
            for i in range(RING):
                step(i, i)
            with eng.Fori(1, TURNS - 1) as j:
                for i in range(RING):
                    step(j * RING + i, i)
            for i in range(RING + 1):
                step((TURNS - 1) * RING + i, i)

        def has(t, lo, hi):
            return not isinstance(t, int) or lo <= t <= hi

        @block.gpsimd
        def _(pool):
            def fetch(t, i):
                i = i % RING
                pool.indirect_dma_start(out=XG[i], out_offset=None, in_=T["x_rows"],
                                        in_offset=bass.IndirectOffsetOnAxis(PICK[i][:, 0:1], 0)).then_inc(x_in[i], 16)
                pool.indirect_dma_start(out=RAW[i], out_offset=None, in_=weights,
                                        in_offset=bass.IndirectOffsetOnAxis(PICK[i][:, 1:2], 0)).then_inc(w_in[i], 16)

            def rest(t, i):
                pool.wait_ge(q["up_hi"], 2 * t + 2)
                gp.tensor_tensor(WL[i % 2][:, PARTS[1]], RAW[i % RING][:, PARTS[1]],
                                 WH[i % 2][:, PARTS[1]].bitcast(F32), ALU.subtract).then_inc(q["up_lo_pool"], 1)

            pool.wait_ge(q["picked"], RING - 1)
            for t in range(RING - 1):
                fetch(t, t)
            rest(0, 0)

            def step(t, i):
                if has(t, 0, SLOT_TILES - RING):
                    pool.wait_ge(q["picked"], t + RING)
                    if has(t, 1, SLOT_TILES):
                        if not isinstance(t, int):
                            pool.sem_inc(q["between"], 1)
                        pool.wait_ge(q["down_lo"], t)
                        if not isinstance(t, int):
                            pool.sem_inc(q["between"], 1)
                        pool.wait_ge(q["up_lo_pool"], t)
                    if not isinstance(t, int):
                        pool.sem_inc(q["between"], 1)
                    fetch(t + RING - 1, i + RING - 1)
                if has(t, 0, SLOT_TILES - 2):
                    rest(t + 1, i + 1)
            run(pool, step)

        @block.sync
        def _(sp):
            def step(t, i):
                if has(t, 1, SLOT_TILES):
                    sp.wait_ge(q["y_taken"], t)
                    if not isinstance(t, int):
                        sp.sem_inc(q["between"], 1)
                    n = (i - 1) % RING
                    rows = slice(P * (t - 1), P * t) if isinstance(t, int) else bass.ds((t - 1) * P, P)
                    sp.dma_start(T["y_rows"][rows], YS[n]).then_inc(y_out[n], 16)
            run(sp, step)
            for n in range(RING):
                sp.wait_ge(y_out[n], 16 * TURNS)

        @block.scalar
        def _(act):
            def turned(t, i):
                act.wait_ge(q["xt_full"], t + 1)
                ac.activation(XTH[i % 2], XT[:], ACT.Copy).then_inc(q["x_hi"], 1)

            def up_weights(t, i, turn):
                act.wait_ge(w_in[i % RING], turn * 16 + 16)
                if has(t, 2, SLOT_TILES):
                    act.wait_ge(q["u_full"], t - 1)
                for part in PARTS:
                    ac.activation(WH[i % 2][:, part], RAW[i % RING][:, part], ACT.Copy).then_inc(q["up_hi"], 1)

            up_weights(0, 0, 0)
            turned(0, 0)

            def step(t, i):
                turn = t // RING if isinstance(t, int) else None
                if has(t, 0, SLOT_TILES - 2):
                    if turn is not None:
                        nxt = (t + 1) // RING
                        act.wait_ge(w_in[(i + 1) % RING], nxt * 16 + 16)
                    else:
                        act.wait_ge(w_in[(i + 1) % RING], (t - i) * (16 // RING) + (16 if i + 1 < RING else 32))
                    if has(t, 1, SLOT_TILES):
                        act.wait_ge(q["u_full"], t)
                    for part in PARTS:
                        ac.activation(WH[(i + 1) % 2][:, part], RAW[(i + 1) % RING][:, part],
                                      ACT.Copy).then_inc(q["up_hi"], 1)
                if has(t, 1, SLOT_TILES):
                    act.wait_ge(q["ht_full"], t)
                    ac.activation(HH[:], HT[:, 0:F], ACT.Copy).then_inc(q["h_hi"], 1)
                if has(t, 0, SLOT_TILES - 2):
                    turned(t + 1, i + 1)
                if has(t, 0, SLOT_TILES - 1):
                    act.wait_ge(q["u_full"], t + 1)
                    ac.activation(SU[i % 2], U[i % 2][:, 0:F], ACT.Silu).then_inc(q["silu_done"], 1)
                    if has(t, 2, SLOT_TILES):
                        act.wait_ge(q["y_full"], t - 1)
                    ac.activation(WH[i % 2][:, DOWN], RAW[i][:, DOWN], ACT.Copy).then_inc(q["down_hi"], 1)
            run(act, step)

        @block.vector
        def _(dve):
            def pick(t, i):
                col = slice(t, t + 1) if isinstance(t, int) else bass.ds(t, 1)
                i = i % RING
                ve.tensor_copy(PICK[i][:, 0:1], T["slot_token"][:, col])
                ve.tensor_copy(PICK[i][:, 1:2], T["weight_row"][:, col]).then_inc(q["picked"], 1)

            def turned_rest(t, i):
                dve.wait_ge(q["x_hi"], t + 1)
                ve.tensor_tensor(XTL[i % 2], XT[:], XTH[i % 2].bitcast(F32), ALU.subtract).then_inc(q["x_lo"], 1)

            def up_rest(t, i):
                dve.wait_ge(q["up_hi"], 2 * t + 1)
                ve.tensor_tensor(WL[i % 2][:, PARTS[0]], RAW[i % RING][:, PARTS[0]],
                                 WH[i % 2][:, PARTS[0]].bitcast(F32), ALU.subtract).then_inc(q["up_lo"], 1)

            for t in range(RING - 1):
                pick(t, t)
            up_rest(0, 0)
            turned_rest(0, 0)

            def step(t, i):
                if has(t, 0, SLOT_TILES - RING):
                    pick(t + RING - 1, i + RING - 1)
                if has(t, 0, SLOT_TILES - 2):
                    up_rest(t + 1, i + 1)
                if has(t, 1, SLOT_TILES):
                    dve.wait_ge(q["h_hi"], t)
                    ve.tensor_tensor(HL[:], HT[:, 0:F], HH[:].bitcast(F32), ALU.subtract).then_inc(q["h_lo"], 1)
                if has(t, 0, SLOT_TILES - 2):
                    turned_rest(t + 1, i + 1)
                if has(t, 0, SLOT_TILES - 1):
                    dve.wait_ge(q["silu_done"], t + 1)
                    ve.tensor_tensor(H[i % 2], SU[i % 2], U[i % 2][:, F:], ALU.mult).then_inc(q["h_made"], 1)
                if has(t, 1, SLOT_TILES):
                    n = (i - 1) % RING
                    dve.wait_ge(q["y_full"], t)
                    if has(t, RING + 1, SLOT_TILES):
                        if isinstance(t, int):
                            dve.wait_ge(y_out[n], 16 * ((t - 1) // RING))
                        else:
                            dve.wait_ge(y_out[n], (t - i) * (16 // RING) - (16 if i == 0 else 0))
                    ve.tensor_copy(YS[n], Y[(i - 1) % 2][:]).then_inc(q["y_taken"], 1)
                if has(t, 0, SLOT_TILES - 1):
                    dve.wait_ge(q["down_hi"], t + 1)
                    ve.tensor_tensor(WL[i % 2][:, DOWN], RAW[i][:, DOWN], WH[i % 2][:, DOWN].bitcast(F32),
                                     ALU.subtract).then_inc(q["down_lo"], 1)
            run(dve, step)

        @block.tensor
        def _(t_):
            def turn_tokens(t, i, count):
                t_.wait_ge(x_in[i % RING], count)
                if has(t, 1, SLOT_TILES):
                    t_.wait_ge(q["x_lo"], t)
                for k in range(KC):
                    last = pe.transpose(XT[:, P * k:P * (k + 1)], XG[i % RING][:, P * k:P * (k + 1)], C["ident"][:])
                last.then_inc(q["xt_full"], 1)

            turn_tokens(0, 0, 16)

            def step(t, i):
                x, w, wl = (XTH[i % 2], XTL[i % 2]), WH[i % 2], WL[i % 2]
                ups = [(xp, wp, k) for xp, wp in ((x[0], w), (x[1], w), (x[0], wl)) for k in range(KC)]

                def up(lo, hi):
                    for n in range(lo, hi):
                        xp, wp, k = ups[n]
                        last = pe.matmul(U[i % 2][:], xp[:, P * k:P * (k + 1)], wp[:, 2 * F * k:2 * F * (k + 1)],
                                         start=(n == 0), stop=(n == len(ups) - 1))
                    return last

                if has(t, 0, SLOT_TILES - 1):
                    t_.wait_ge(q["up_lo"], t + 1)
                    t_.wait_ge(q["x_lo"], t + 1)
                    if has(t, 2, SLOT_TILES):
                        t_.wait_ge(q["h_made"], t - 1)
                    up(0, 8)
                if has(t, 1, SLOT_TILES):
                    t_.wait_ge(q["h_made"], t)
                    if has(t, 2, SLOT_TILES):
                        t_.wait_ge(q["h_lo"], t - 1)
                    for h in range(2):
                        last = pe.transpose(HT[:, P * h:P * (h + 1)], H[(i - 1) % 2][:, P * h:P * (h + 1)], C["ident"][:])
                    last.then_inc(q["ht_full"], 1)
                if has(t, 0, SLOT_TILES - 1):
                    t_.wait_ge(q["up_lo_pool"], t + 1)
                    up(8, 12).then_inc(q["u_full"], 1)
                if has(t, 0, SLOT_TILES - 2):
                    if isinstance(t, int):
                        turn_tokens(t + 1, i + 1, 16 * ((t + 1) // RING + 1))
                    else:
                        turn_tokens(t + 1, i + 1, (t - i) * (16 // RING) + (16 if i + 1 < RING else 32))
                if has(t, 1, SLOT_TILES):
                    t_.wait_ge(q["h_lo"], t)
                    t_.wait_ge(q["down_lo"], t)
                    if has(t, 3, SLOT_TILES):
                        t_.wait_ge(q["y_taken"], t - 2)
                    n = 0
                    r = (i - 1) % 2
                    for hp, wp in ((HH, WH[r]), (HL, WH[r]), (HH, WL[r])):
                        for h in range(2):
                            last = pe.matmul(Y[r][:], hp[:, P * h:P * (h + 1)], wp[:, UGW + D * h:UGW + D * (h + 1)],
                                             start=(n == 0), stop=(n == 5))
                            n += 1
                    last.then_inc(q["y_full"], 1)
            run(t_, step)


def combine_slots(nc, X, T):
    NTILE, RING = NB * NT, 4
    ve = nc.vector
    ctx = ExitStack()
    with ctx:
        sb = lambda n, s, d: ctx.enter_context(nc.sbuf_tensor(f"combine_{n}", s, d))
        sem = own_semaphores(nc, ctx, f"combine")
        XF = X[:].rearrange("p b i d -> p (b i) d")
        YG = [sb(f"YG{i}", [P, 2, D], F32) for i in range(RING)]
        stats = sb("stats", [P, NTILE, 6], F32)
        mean, var, rstd, tmp = (sb(n, [P, NTILE], F32) for n in ("mean", "var", "rstd", "tmp"))
        added, stat, norm = sem("added"), sem("stat"), sem("norm")
        y_in = [sem(f"y_in{i}") for i in range(RING)]
        block = ctx.enter_context(nc.Block())

        @block.gpsimd
        def _(pool):
            for t in range(NTILE):
                if t >= RING:
                    pool.wait_ge(added, 2 * (t - RING) + 2)
                for k in range(2):
                    pool.indirect_dma_start(out=YG[t % RING][:, k, :], out_offset=None, in_=T["y_rows"],
                                            in_offset=bass.IndirectOffsetOnAxis(T["slot"][:, k, t:t + 1], 0)
                                            ).then_inc(y_in[t % RING], 16)

        @block.vector
        def _(dve):
            for t in range(NTILE):
                dve.wait_ge(y_in[t % RING], 32 * (t // RING + 1))
                for k in range(2):
                    ve.scalar_tensor_tensor(out=XF[:, t, :], in0=YG[t % RING][:, k, :], scalar=T["share"][:, k, t:t + 1],
                                            in1=XF[:, t, :], op0=ALU.mult, op1=ALU.add).then_inc(added, 1)
                    dve.wait_ge(added, 2 * t + k + 1)
                ve.bn_stats(stats[:, t, :], XF[:, t, :]).then_inc(stat, 1)
            dve.wait_ge(stat, NTILE)
            fin = Steps(dve, norm, 0, RSTD_STEPS + NTILE)
            emit_rstd(nc, fin, stats[:], mean[:], var[:], rstd[:], tmp[:])
            for t in range(NTILE):
                fin(ve.tensor_scalar(XF[:, t, :], XF[:, t, :], mean[:, t:t + 1], rstd[:, t:t + 1],
                                     ALU.subtract, ALU.mult))
            fin.done()


def make_constants(nc, ctx):
    sb = lambda n, s, d: ctx.enter_context(nc.sbuf_tensor(n, s, d))
    C = dict(ident=sb("ident", [P, P], F32), identr=sb("identr", [P, P], F32R),
             identb=sb("identb", [P, P], BF16),
             mask_qk=sb("mask_qk", [P, P], F32R), mask_kq=sb("mask_kq", [P, P], F32R))
    with ExitStack() as c2:
        mk = c2.enter_context(nc.sbuf_tensor("mask_tmp", [P, 2, P], F32))
        made = c2.enter_context(nc.semaphore("made"))
        copied = c2.enter_context(nc.semaphore("copied"))
        block = c2.enter_context(nc.Block())

        @block.gpsimd
        def _(pool):
            pool.memset(C["ident"][:], 0.0).then_inc(made, 1)
            pool.memset(mk[:], 0.0).then_inc(made, 1)
            pool.wait_ge(made, 2)
            pool.affine_select(out=C["ident"][:], in_=C["ident"][:], compare_op=ALU.not_equal, fill=1.0,
                               base=0, pattern=[[-1, P]], channel_multiplier=1).then_inc(made, 1)
            pool.affine_select(out=mk[:, 0, :], in_=mk[:, 0, :], compare_op=ALU.is_ge, fill=NEG,
                               base=0, pattern=[[-1, P]], channel_multiplier=1).then_inc(made, 1)
            pool.affine_select(out=mk[:, 1, :], in_=mk[:, 1, :], compare_op=ALU.is_ge, fill=NEG,
                               base=0, pattern=[[1, P]], channel_multiplier=-1).then_inc(made, 1)

        @block.vector
        def _(dve):
            dve.wait_ge(made, 5)
            nc.vector.tensor_copy(C["identr"][:], C["ident"][:])
            nc.vector.tensor_copy(C["identb"][:], C["ident"][:])
            nc.vector.tensor_copy(C["mask_qk"][:], mk[:, 0, :])
            nc.vector.tensor_copy(C["mask_kq"][:], mk[:, 1, :])
    return C


def load_x(nc, X, x):
    with nc.semaphore("x_in") as x_in, nc.Block() as block:
        @block.sync
        def _(sp):
            sp.dma_start(X[:], x).then_inc(x_in, 16)
            sp.wait_ge(x_in, 16)


def store_x(nc, X, out):
    with nc.semaphore("x_out") as x_out, nc.Block() as block:
        @block.sync
        def _(sp):
            sp.dma_start(out, X[:]).then_inc(x_out, 16)
            sp.wait_ge(x_out, 16)


def build(nc, A, out, stages="ABFCEM"):
    ctx = ExitStack()
    with ctx:
        X = ctx.enter_context(nc.sbuf_tensor("X", [P, NB, NT, D], F32))
        load_x(nc, X, A["x"].rearrange("b (i p) d -> p b i d", p=P))
        C = make_constants(nc, ctx)
        for s in stages:
            if s in "AC":
                l = "L0_attn" if s == "A" else "L1_attn"
                stage_self_attention(nc, l, X, C, [A[f"{l}_W{w}T"].rearrange("(k p) n -> p k n", p=P) for w in "qkvo"],
                                     A[f"{l}_bqk"], A[f"{l}_rows"])
            if s == "B":
                stage_cross_attention(nc, X, C, A)
            if s == "F":
                stage_ffn(nc, X, C, A)
            if s == "E":
                stage_graph(nc, X, C, A)
            if s == "M":
                stage_experts(nc, X, C, A)
        store_x(nc, X, out.rearrange("b (i p) d -> p b i d", p=P))


def layout(inputs):
    import numpy as np
    A = {}
    as_np = {k: np.asarray(v) for k, v in inputs.items()}
    A["x"] = as_np["x"]
    for l in ("L0_attn", "L1_attn"):
        for w in "qkvo":
            A[f"{l}_W{w}T"] = as_np[f"{l}_W{w}"].T
        A[f"{l}_bqk"] = np.stack([as_np[f"{l}_b{w}"].reshape(KC, P).T for w in "qk"], axis=1)
        A[f"{l}_rows"] = np.stack([np.broadcast_to(as_np[f"{l}_b{w}"], (P, D)) for w in "vo"], axis=1)
    for w in ("gate", "up", "down"):
        A[f"w_{w}T"] = as_np[f"L0_ffn_w_{w}"].T
    h2 = np.array([[1, 1], [1, -1]], np.float32)
    h4, h128 = np.kron(h2, h2), h2
    for _ in range(6):
        h128 = np.kron(h128, h2)
    A["signs"] = (h128[:, None, None, :] * h4[None, :, :, None]).reshape(P, 4 * BANK)
    A["graph_w"] = np.stack([as_np[f"L1_xattn_W{w}"].T for w in "qk"], axis=1)
    A["gamma"] = np.broadcast_to(as_np["L1_xattn_gamma_raw"].reshape(1, 1), (P, 1))
    A["router_wT"] = as_np["L1_ffn_router_w"].T
    A["router_b"] = np.broadcast_to(as_np["L1_ffn_router_bias"], (P, NB * NT, 16))
    up, gate = (np.concatenate([as_np[f"L1_ffn_W{w}"], as_np[f"L1_ffn_S{w}"].reshape(D, 2, 256).transpose(1, 0, 2)])
                for w in "ug")
    up_gate = np.concatenate([up, gate], axis=2)
    down = np.concatenate([as_np["L1_ffn_Wd"], as_np["L1_ffn_Sd"].reshape(2, 256, D)])
    A["experts"] = np.concatenate([w.reshape(18, -1, P, w.shape[2]).transpose(0, 2, 1, 3).reshape(18, P, -1)
                                   for w in (up_gate, down)], axis=2)
    A["ctx_512"] = as_np["ctx_512"]
    A["ctxT"] = as_np["ctx_512"].transpose(0, 2, 1)
    return {k: np.ascontiguousarray(v) for k, v in A.items()}


def kernel(**inputs):
    import numpy as _np
    import concourse.bacc as _bacc
    from concourse.bass_utils import run_bass_kernel_spmd as _run

    nc = _bacc.Bacc("TRN2", target_bir_lowering=False, num_devices=1)
    arrays = layout(inputs)
    args = {k: nc.dram_tensor(f"in_{k}", a.shape, mybir.dt.from_np(a.dtype), kind="ExternalInput").ap()
            for k, a in arrays.items()}
    out = nc.dram_tensor("out_x", (NB, S, D), F32, kind="ExternalOutput").ap()
    build(nc, args, out)
    r = _run(nc, [{f"in_{k}": a for k, a in arrays.items()}], core_ids=[0])
    return r.results[0]["out_x"]
```
